# Optimizing a Trainium2 kernel written in Bass

```python
import numpy as np
import jax
import jax.numpy as jnp

def _softmax(x, axis=-1):
    return jax.nn.softmax(x, axis=axis)

def _gelu(x):
    return jax.nn.gelu(x, approximate=True)

def _silu(x):
    return jax.nn.silu(x)

def _sigmoid(x):
    return jax.nn.sigmoid(x)

def _layernorm(x, axis=-1, eps=1e-05):
    m = jnp.mean(x, axis=axis, keepdims=True)
    v = jnp.var(x, axis=axis, keepdims=True)
    return (x - m) / jnp.sqrt(v + eps)

def _scatter_add(tgt, idx, src, axis=0):
    return tgt.at[idx].add(src)

def _segment_sum(src, seg, n):
    return jax.ops.segment_sum(src, seg, n)
kernel_name = 'mk_decoder_postln_d1_seqx_r8_ac1e94'

def setup_inputs(seed: int=0):
    np.random.seed(seed)
    _w = jnp.asarray

    def _rec_inputs():
        import jax
        import jax.numpy as jnp
        _rk = jax.random.key(seed)
        x = -0.0003929 + 0.9999 * jax.random.normal(jax.random.fold_in(_rk, 1), (128, 64, 128), jnp.float32)
        _lenS = 64 - jax.random.randint(jax.random.fold_in(_rk, 7), (128,), 0, max(1, 64 // 4) + 1, jnp.int32)
        _lenS2 = 64 - jax.random.randint(jax.random.fold_in(_rk, 8), (128,), 0, max(1, 64 // 4) + 1, jnp.int32)
        _ctx_1024P = jax.random.normal(jax.random.fold_in(_rk, 11), (128, 16, 128), jnp.float32)
        _ctx_1024c = jax.random.dirichlet(jax.random.fold_in(_rk, 511), 0.3 * jnp.ones((16,), jnp.float32), (128, 64))
        _ctx_1024t = jnp.einsum('bsk,bkd->bsd', _ctx_1024c, _ctx_1024P)
        _ctx_1024t = _ctx_1024t * jax.lax.rsqrt(jnp.mean(jnp.square(_ctx_1024t)) + 1e-12) * 0.953939
        ctx_1024 = 2.81802e-05 + 1.00001 * (_ctx_1024t + 0.3 * jax.random.normal(jax.random.fold_in(_rk, 611), (128, 64, 128), jnp.float32))
        return (x, ctx_1024)
    x, ctx_1024 = _rec_inputs()

    def _L0_attn_setup():
        import jax, jax.numpy as jnp
        import numpy as np
        from jax import lax
        B, S, E, H, KS = (2, 256, 128, 16, 3)
        DH = E // H
        key = jax.random.key(seed)
        ks = jax.random.split(key, 11)
        s = 1.0 / np.sqrt(E)
        sc = 1.0 / np.sqrt(H * KS)
        return {'query': jax.random.normal(ks[0], (B, S, E), jnp.float32), 'Wq': jax.random.uniform(ks[1], (E, E), jnp.float32, -s, s), 'bq': jax.random.uniform(ks[2], (E,), jnp.float32, -s, s), 'Wk': jax.random.uniform(ks[3], (E, E), jnp.float32, -s, s), 'bk': jax.random.uniform(ks[4], (E,), jnp.float32, -s, s), 'Wv': jax.random.uniform(ks[5], (E, E), jnp.float32, -s, s), 'bv': jax.random.uniform(ks[6], (E,), jnp.float32, -s, s), 'Wo': jax.random.uniform(ks[7], (E, E), jnp.float32, -s, s), 'bo': jax.random.uniform(ks[8], (E,), jnp.float32, -s, s), 'conv_w': jax.random.uniform(ks[9], (H, H, KS), jnp.float32, -sc, sc), 'conv_b': jax.random.uniform(ks[10], (H,), jnp.float32, -sc, sc)}
    _L0_attn_all = _L0_attn_setup()
    _L0_attn_in = {k: v for k, v in _L0_attn_all.items() if k in ('Wq', 'bq', 'Wk', 'bk', 'Wv', 'bv', 'Wo', 'bo', 'conv_w', 'conv_b')}
    del _L0_attn_all

    def _L0_xattn_setup():
        import jax, jax.numpy as jnp
        import numpy as np
        key = jax.random.key(seed)
        ks = jax.random.split(key, 9)
        B, S, D = (8, 256, 128)
        Qd = Kd = Vd = 128
        s = 1.0 / np.sqrt(D)
        return {'query': jax.random.normal(ks[0], (B, S, D), jnp.float32), 'key': jax.random.normal(ks[1], (B, S, D), jnp.float32), 'value': jax.random.normal(ks[2], (B, S, D), jnp.float32), 'Wq': jax.random.normal(ks[3], (D, Qd), jnp.float32) * s, 'bq': jnp.zeros((Qd,), jnp.float32), 'Wk': jax.random.normal(ks[4], (D, Kd), jnp.float32) * s, 'bk': jnp.zeros((Kd,), jnp.float32), 'Wv': jax.random.normal(ks[5], (D, Vd), jnp.float32) * s, 'bv': jnp.zeros((Vd,), jnp.float32)}
    _L0_xattn_all = _L0_xattn_setup()
    _L0_xattn_in = {k: v for k, v in _L0_xattn_all.items() if k in ('Wq', 'bq', 'Wk', 'bk', 'Wv', 'bv')}
    del _L0_xattn_all

    def _L0_ffn_setup():
        import jax, jax.numpy as jnp
        import numpy as np
        B, S, H = (4, 256, 128)
        F = 512
        E = 8
        JITTER_EPS = 0.01

        def _sparse_mixer_top2(scores, jitter_eps):
            vals, idx = jax.lax.top_k(scores, 2)
            neg_inf = -jnp.inf
            m1 = vals[:, :1]
            factor1 = jnp.maximum(jnp.abs(scores), m1)
            mask1 = (m1 - scores) / factor1 > 2 * jitter_eps
            p1 = jax.nn.softmax(jnp.where(mask1, neg_inf, scores), axis=-1)
            mult1 = jnp.take_along_axis(p1, idx[:, :1], axis=-1)[:, 0]
            m2 = vals[:, 1:2]
            factor2 = jnp.maximum(jnp.abs(scores), m2)
            mask2 = (m2 - scores) / factor2 > 2 * jitter_eps
            top1_onehot = jnp.arange(scores.shape[-1])[None, :] == idx[:, :1]
            s2 = jnp.where(top1_onehot, neg_inf, scores)
            p2 = jax.nn.softmax(jnp.where(mask2, neg_inf, s2), axis=-1)
            mult2 = jnp.take_along_axis(p2, idx[:, 1:2], axis=-1)[:, 0]
            return (mult1, mult2, idx)
        key = jax.random.key(seed)
        k0, k1, k2, k3, k4 = jax.random.split(key, 5)
        hidden_states = jax.random.normal(k0, (B, S, H), dtype=jnp.float32)
        gate_w = jax.random.normal(k1, (E, H), dtype=jnp.float32) * 0.02
        w1 = jax.random.normal(k2, (E, F, H), dtype=jnp.float32) * 0.02
        w2 = jax.random.normal(k3, (E, H, F), dtype=jnp.float32) * 0.02
        w3 = jax.random.normal(k4, (E, F, H), dtype=jnp.float32) * 0.02
        return {'hidden_states': hidden_states, 'gate_w': gate_w, 'w1': w1, 'w2': w2, 'w3': w3}
    _L0_ffn_all = _L0_ffn_setup()
    _L0_ffn_in = {k: v for k, v in _L0_ffn_all.items() if k in ('gate_w', 'w1', 'w2', 'w3')}
    del _L0_ffn_all
    return {'x': x, 'ctx_1024': ctx_1024, 'L0_attn_Wq': _L0_attn_in['Wq'], 'L0_attn_bq': _L0_attn_in['bq'], 'L0_attn_Wk': _L0_attn_in['Wk'], 'L0_attn_bk': _L0_attn_in['bk'], 'L0_attn_Wv': _L0_attn_in['Wv'], 'L0_attn_bv': _L0_attn_in['bv'], 'L0_attn_Wo': _L0_attn_in['Wo'], 'L0_attn_bo': _L0_attn_in['bo'], 'L0_attn_conv_w': _L0_attn_in['conv_w'], 'L0_attn_conv_b': _L0_attn_in['conv_b'], 'L0_xattn_Wq': _L0_xattn_in['Wq'], 'L0_xattn_bq': _L0_xattn_in['bq'], 'L0_xattn_Wk': _L0_xattn_in['Wk'], 'L0_xattn_bk': _L0_xattn_in['bk'], 'L0_xattn_Wv': _L0_xattn_in['Wv'], 'L0_xattn_bv': _L0_xattn_in['bv'], 'L0_ffn_gate_w': _L0_ffn_in['gate_w'], 'L0_ffn_w1': _L0_ffn_in['w1'], 'L0_ffn_w2': _L0_ffn_in['w2'], 'L0_ffn_w3': _L0_ffn_in['w3']}

def reference(x, ctx_1024, L0_attn_Wq, L0_attn_bq, L0_attn_Wk, L0_attn_bk, L0_attn_Wv, L0_attn_bv, L0_attn_Wo, L0_attn_bo, L0_attn_conv_w, L0_attn_conv_b, L0_xattn_Wq, L0_xattn_bq, L0_xattn_Wk, L0_xattn_bk, L0_xattn_Wv, L0_xattn_bv, L0_ffn_gate_w, L0_ffn_w1, L0_ffn_w2, L0_ffn_w3):
    import jax
    import jax.numpy as jnp

    def _L0_attn_ref(query, Wq, bq, Wk, bk, Wv, bv, Wo, bo, conv_w, conv_b):
        import jax, jax.numpy as jnp
        import numpy as np
        from jax import lax
        B, S, E, H, KS = (2, 256, 128, 16, 3)
        DH = E // H
        b, s, e = query.shape
        h, dh = (H, DH)
        Q = (query @ Wq.T + bq).reshape(b, s, h, dh).transpose(0, 2, 1, 3)
        K = (query @ Wk.T + bk).reshape(b, s, h, dh).transpose(0, 2, 1, 3)
        V = (query @ Wv.T + bv).reshape(b, s, h, dh).transpose(0, 2, 1, 3)
        scores = jnp.einsum('bhqd,bhkd->bhqk', Q, K) / np.sqrt(dh).astype(np.float32)
        x = scores.transpose(0, 2, 1, 3).reshape(b * s, h, s)
        x = lax.conv_general_dilated(x, conv_w, window_strides=(1,), padding=[(KS // 2, KS // 2)], dimension_numbers=('NCW', 'OIW', 'NCW'))
        x = x + conv_b[None, :, None]
        scores = x.reshape(b, s, h, s).transpose(0, 2, 1, 3)
        weights = jax.nn.softmax(scores, axis=-1)
        out = jnp.einsum('bhqk,bhkd->bqhd', weights, V).reshape(b, s, e)
        return out @ Wo.T + bo

    def _L0_xattn_ref(query, key, value, Wq, bq, Wk, bk, Wv, bv):
        import jax, jax.numpy as jnp
        import numpy as np
        Q = jnp.einsum('bsd,de->bse', query, Wq) + bq
        K = jnp.einsum('bsd,de->bse', key, Wk) + bk
        V = jnp.einsum('bsd,de->bse', value, Wv) + bv
        scale = 1.0 / jnp.sqrt(jnp.asarray(K.shape[-1], Q.dtype))
        scores = jnp.einsum('bqe,bke->bqk', Q, K) * scale
        attn = jax.nn.softmax(scores, axis=-1)
        return jnp.einsum('bqk,bkv->bqv', attn, V)

    def _L0_ffn_ref(hidden_states, gate_w, w1, w2, w3):
        import jax, jax.numpy as jnp
        import numpy as np
        B, S, H = (4, 256, 128)
        F = 512
        E = 8
        JITTER_EPS = 0.01

        def _sparse_mixer_top2(scores, jitter_eps):
            vals, idx = jax.lax.top_k(scores, 2)
            neg_inf = -jnp.inf
            m1 = vals[:, :1]
            factor1 = jnp.maximum(jnp.abs(scores), m1)
            mask1 = (m1 - scores) / factor1 > 2 * jitter_eps
            p1 = jax.nn.softmax(jnp.where(mask1, neg_inf, scores), axis=-1)
            mult1 = jnp.take_along_axis(p1, idx[:, :1], axis=-1)[:, 0]
            m2 = vals[:, 1:2]
            factor2 = jnp.maximum(jnp.abs(scores), m2)
            mask2 = (m2 - scores) / factor2 > 2 * jitter_eps
            top1_onehot = jnp.arange(scores.shape[-1])[None, :] == idx[:, :1]
            s2 = jnp.where(top1_onehot, neg_inf, scores)
            p2 = jax.nn.softmax(jnp.where(mask2, neg_inf, s2), axis=-1)
            mult2 = jnp.take_along_axis(p2, idx[:, 1:2], axis=-1)[:, 0]
            return (mult1, mult2, idx)
        Bv, Sv, Hv = hidden_states.shape
        x = hidden_states.reshape(-1, Hv)
        scores = x @ gate_w.T
        mult1, mult2, idx = _sparse_mixer_top2(scores, JITTER_EPS)
        out = jnp.zeros_like(x)
        for e in range(E):
            w_tok = mult1 * (idx[:, 0] == e) + mult2 * (idx[:, 1] == e)
            h = jax.nn.silu(x @ w1[e].T) * (x @ w3[e].T)
            out = out + w_tok[:, None] * (h @ w2[e].T)
        return out.reshape(Bv, Sv, Hv)
    x = _layernorm(x + _L0_attn_ref(x, L0_attn_Wq, L0_attn_bq, L0_attn_Wk, L0_attn_bk, L0_attn_Wv, L0_attn_bv, L0_attn_Wo, L0_attn_bo, L0_attn_conv_w, L0_attn_conv_b), axis=-1)
    x = _layernorm(x + _L0_xattn_ref(x, ctx_1024, ctx_1024, L0_xattn_Wq, L0_xattn_bq, L0_xattn_Wk, L0_xattn_bk, L0_xattn_Wv, L0_xattn_bv), axis=-1)
    x = _layernorm(x + _L0_ffn_ref(x, L0_ffn_gate_w, L0_ffn_w1, L0_ffn_w2, L0_ffn_w3), axis=-1)
    return x

_drawn_inputs = setup_inputs


def setup_inputs(seed=0):
    import zlib

    import numpy as np

    out = dict(_drawn_inputs(seed))
    spreads = {'L0_xattn_bq': (0.0, 0.347), 'L0_xattn_bk': (0.0, 0.8), 'L0_xattn_bv': (0.0, 0.1)}
    factors = {'L0_attn_Wq': 7.275,
     'L0_attn_bq': 8.0,
     'L0_attn_Wk': 7.257,
     'L0_attn_bk': 8.0,
     'L0_attn_conv_w': 7.357,
     'L0_attn_conv_b': 8.0,
     'L0_ffn_gate_w': 4.0,
     'L0_ffn_w1': 3.487,
     'L0_ffn_w2': 3.482,
     'L0_ffn_w3': 3.477}
    for name, (base, spread) in spreads.items():
        noise = np.random.default_rng([zlib.crc32(name.encode()), seed]).standard_normal(out[name].shape)
        drawn = base * np.exp(spread * noise) if base else spread * noise
        out[name] = jnp.asarray(drawn.astype(out[name].dtype))
    for name, factor in factors.items():
        out[name] = (out[name] * factor).astype(out[name].dtype)
    return out
```

```python
from contextlib import ExitStack

import numpy as np

import concourse.bass as bass
from concourse import mybir

F32 = mybir.dt.float32
U32 = mybir.dt.uint32
ALU = mybir.AluOpType
ACT = mybir.ActivationFunctionType
AX = mybir.AxisListType

B, S, D = 128, 64, 128
H, DH, KS = 16, 8, 3
E, F = 8, 512
P = 128
T = B * S // P
BT = P // S
PAIRS = H // 2
EPS = 1e-5
JITTER = 0.01


def need(engine, semaphore, value):
    if not (isinstance(value, int) and value <= 0):
        engine.wait_ge(semaphore, value)


def skewed(engine, units, lag, body):
    for i in range(lag):
        body(i, i % 2)
    with engine.Fori(lag // 2, units // 2) as two:
        for p in range(2):
            body(2 * two + p, p)
    for i in range(units, units + lag):
        body(i, i % 2)


def upto(count, units):
    return min(count, units) if isinstance(count, int) else count


def stage(i, lag, units):
    u = i - lag
    if isinstance(i, int) and not 0 <= u < units:
        return None
    return u


def self_attention(nc, sb, ps, consts, dram, x_all):
    UNITS = T // 2
    NB = 2 * BT
    scale = 1.0 / float(np.sqrt(np.float32(DH)))

    with ExitStack() as ctx:
        def tile(name, shape, dt=F32):
            return ctx.enter_context(nc.sbuf_tensor(name, shape, dt))

        def sem(name):
            return ctx.enter_context(nc.semaphore(name))

        x_in = [tile(f"x_in{p}", [P, 2, D]) for p in range(2)]
        xT = [tile(f"xT{p}", [P, 2 * P]) for p in range(2)]
        qT = [tile(f"qT{p}", [P, 2 * P]) for p in range(2)]
        kpad = [tile(f"kpad{p}", [P, NB, S + 2]) for p in range(2)]
        kc = [tile(f"kc{p}", [P, NB, H, S]) for p in range(2)]
        vbd = [tile(f"vbd{p}", [P, PAIRS, NB, 2, DH]) for p in range(2)]
        probs = [tile(f"probs{s}", [P, H, S]) for s in range(2)]
        probsT = [tile(f"probsT{s}", [P, PAIRS, P]) for s in range(2)]
        rsum = [tile(f"rsum{s}", [P, 2 * P]) for s in range(2)]
        outT = [tile(f"outT{s}", [P, 2, P]) for s in range(2)]
        top = [tile(f"top{s}", [P, H]) for s in range(2)]
        topb = [tile(f"topb{s}", [P, H]) for s in range(2)]
        shift = [tile(f"shift{s}", [P, H]) for s in range(2)]
        res = tile("res", [P, 2, D])
        stats = tile("stats", [P, 2, 6])
        mv = tile("mv", [P, 2, 2])
        veps = tile("veps", [P, 2])
        rstd = tile("rstd", [P, 2])

        ps_s = [ps[:, 2 * s:2 * s + 2, :] for s in range(2)]
        ps_pt = ps[:, 4, :]
        ps_qk = ps[:, 5, :]
        ps_vo = ps[:, 6, :]
        ps_x = ps[:, 7, 0:256]
        ps_a = ps[:, 7, 256:512].rearrange("p (s e) -> p s e", s=2)

        x_landed = [sem(f"x_landed{p}") for p in range(2)]
        xb_done = sem("xb_done")
        xT_mm, xT_sb = sem("xT_mm"), sem("xT_sb")
        qk_mm, q_sb, k_sb = sem("qk_mm"), sem("q_sb"), sem("k_sb")
        v_mm, v_sb = sem("v_mm"), sem("v_sb")
        tap_done, mid_done, conv_done = sem("tap_done"), sem("mid_done"), sem("conv_done")
        s_mm = [sem(f"s_mm{s}") for s in range(2)]
        top_done = [sem(f"top_done{s}") for s in range(2)]
        topb_done = [sem(f"topb_done{s}") for s in range(2)]
        shift_done = [sem(f"shift_done{s}") for s in range(2)]
        sub_done = [sem(f"sub_done{s}") for s in range(2)]
        exp_done = [sem(f"exp_done{s}") for s in range(2)]
        pt_mm, pt_sb = sem("pt_mm"), sem("pt_sb")
        o_mm = [sem(f"o_mm{s}") for s in range(2)]
        rsum_done = [sem(f"rsum_done{s}") for s in range(2)]
        o_sb = [sem(f"o_sb{s}") for s in range(2)]
        a_mm = [sem(f"a_mm{s}") for s in range(2)]
        res_done, mv_done = sem("res_done"), sem("mv_done")
        veps_done, rstd_done, x1_done = sem("veps_done"), sem("rstd_done"), sem("x1_done")
        zeroed = sem("zeroed")

        x_tiles = dram["x"].rearrange("(t b) s e -> (b s) t e", b=BT)
        block = ctx.enter_context(nc.Block())

        @block.sync
        def _(sp):
            def load(u, p):
                need(sp, xT_mm, u - 1)
                need(sp, xb_done, u - 1)
                sp.dma_start(x_in[p][:], x_tiles[:, bass.ds(2 * u, 2), :]).then_inc(x_landed[p], 16)

            for p in range(2):
                load(p, p)
            with sp.Fori(1, UNITS // 2) as two:
                for p in range(2):
                    load(2 * two + p, p)

        @block.gpsimd
        def _(pool):
            for p in range(2):
                nc.gpsimd.memset(kpad[p][:], 0.0).then_inc(zeroed, 1)
                nc.gpsimd.memset(vbd[p][:], 0.0).then_inc(zeroed, 1)

            def residual_in(u, p):
                pool.wait_ge(x_landed[p], 8 * (u - p) + 16)
                nc.gpsimd.tensor_tensor(x_all[:, bass.ds(2 * u, 2), :], x_in[p][:],
                                        consts["bo"].unsqueeze(1).to_broadcast([P, 2, D]),
                                        ALU.add).then_inc(xb_done, 1)

            def rsqrt(w):
                pool.wait_ge(mv_done, w + 1)
                nc.gpsimd.tensor_tensor(veps[:], mv[:, :, 1], consts["eps"][:, 0:mv.shape[1]], ALU.add).then_inc(veps_done, 1)
                pool.wait_ge(veps_done, w + 1)
                nc.gpsimd.tensor_tensor(rstd[:], veps[:], consts["mhalf"][:, 0:2], ALU.pow).then_inc(rstd_done, 1)

            def body(i, p):
                if (u := stage(i, 0, UNITS)) is not None:
                    residual_in(u, p)
                if (w := stage(i, 2, UNITS)) is not None:
                    rsqrt(w)

            skewed(pool, UNITS, 2, body)

        @block.tensor
        def _(pe):
            ident = consts["ident"]

            def x_transposes(u, p):
                pe.wait_ge(x_landed[p], 8 * (u - p) + 16)
                need(pe, xT_sb, u)
                need(pe, res_done, u - 2)
                for s in range(2):
                    last = nc.tensor.transpose(ps_x[:, s * P:(s + 1) * P], x_in[p][:, s, :], ident[:])
                last.then_inc(xT_mm, 1)

            def qk_products(u, p):
                pe.wait_ge(xT_sb, u + 1)
                need(pe, k_sb, u)
                nc.tensor.matmul(ps_qk[:, 0:256], consts["wqT"][:], xT[p][:], start=True, stop=True)
                nc.tensor.matmul(ps_qk[:, 256:512], consts["wkT"][:], xT[p][:],
                                 start=True, stop=True).then_inc(qk_mm, 1)

            def v_products(u, p):
                need(pe, v_sb, u)
                need(pe, o_sb[1], u - 1)
                for b in range(NB):
                    for h in range(2):
                        last = nc.tensor.matmul(ps_vo[64 * h:64 * h + 64, b * D:(b + 1) * D],
                                                xT[p][:, b * S:(b + 1) * S], consts["wvT"][:],
                                                start=True, stop=True)
                last.then_inc(v_mm, 1)

            def scores(w, p, s):
                if s == 0:
                    pe.wait_ge(q_sb, w + 1)
                    pe.wait_ge(conv_done, 4 * w + 4)
                need(pe, sub_done[s], w)
                for half in range(2):
                    for b in range(BT):
                        last = nc.tensor.matmul(
                            ps_s[s][64 * b:64 * b + 64, half, :],
                            qT[p][:, s * P + b * S:s * P + (b + 1) * S],
                            kc[p][:, BT * s + b, 8 * half:8 * half + 8, :], start=True, stop=True)
                last.then_inc(s_mm[s], 1)

            def p_transposes(w, s):
                pe.wait_ge(exp_done[s], w + 1)
                for g in range(2):
                    need(pe, pt_sb, 4 * w + 2 * s + g)
                    for j in range(4):
                        last = nc.tensor.transpose(ps_pt[:, j * P:(j + 1) * P],
                                                   probs[s][:, 8 * g + 2 * j:8 * g + 2 * j + 2, :], ident[:])
                    last.then_inc(pt_mm, 1)

            def outputs(w, p, s):
                pe.wait_ge(pt_sb, 4 * w + 2 * s + 2)
                if s == 0:
                    pe.wait_ge(v_sb, upto(w + 2, UNITS))
                else:
                    pe.wait_ge(o_sb[0], w + 1)
                for j in range(PAIRS):
                    q = slice(32 * (j % 4), 32 * (j % 4) + 32)
                    for n, left in enumerate((vbd[p][:, j, BT * s:BT * s + BT, :, :], consts["pair_ones"][:])):
                        c = (2 * n + j // 4) * P
                        last = nc.tensor.matmul(ps_vo[q, c:c + P], left, probsT[s][:, j, :],
                                                start=True, stop=True, tile_position=(0, 32 * (j % 4)))
                last.then_inc(o_mm[s], 1)

            def projection(w, s):
                pe.wait_ge(o_sb[s], w + 1)
                pe.wait_ge(xT_sb, upto(w + 3, UNITS))
                for half in range(2):
                    for b in range(BT):
                        last = nc.tensor.matmul(ps_a[64 * b:64 * b + 64, s, :],
                                                outT[s][:, half, b * S:(b + 1) * S],
                                                consts["woP"][:, b, half, :],
                                                start=(half == 0), stop=(half == 1))
                last.then_inc(a_mm[s], 1)

            def body(i, p):
                u, w = stage(i, 0, UNITS), stage(i, 2, UNITS)
                if u is not None:
                    x_transposes(u, p)
                if w is not None:
                    scores(w, p, 0)
                    scores(w, p, 1)
                if u is not None:
                    qk_products(u, p)
                if w is not None:
                    p_transposes(w, 0)
                    outputs(w, p, 0)
                    p_transposes(w, 1)
                    outputs(w, p, 1)
                    projection(w, 0)
                    projection(w, 1)
                if u is not None:
                    v_products(u, p)

            skewed(pe, UNITS, 2, body)

        @block.scalar
        def _(act):
            act.wait_ge(zeroed, 4)

            def copy_xT(u, p):
                act.wait_ge(xT_mm, u + 1)
                need(act, v_mm, u - 1)
                nc.scalar.copy(xT[p][:], ps_x).then_inc(xT_sb, 1)

            def copy_qk(u, p):
                act.wait_ge(qk_mm, u + 1)
                need(act, s_mm[1], u - 1)
                need(act, conv_done, 4 * (u - 1))
                nc.scalar.activation(qT[p][:], ps_qk[:, 0:256], ACT.Identity, bias=consts["bq"][:],
                                     scale=scale).then_inc(q_sb, 1)
                nc.scalar.activation(kpad[p][:, :, 1:S + 1],
                                     ps_qk[:, 256:512].rearrange("p (b k) -> p b k", b=NB), ACT.Identity,
                                     bias=consts["bk"][:]).then_inc(k_sb, 1)

            def tap(u, p, g):
                if g == 0:
                    act.wait_ge(k_sb, u + 1)
                    need(act, s_mm[1], u - 1)
                for o in range(4 * g, 4 * g + 4):
                    last = nc.scalar.activation(kc[p][:, :, o, :], kpad[p][:, :, 0:S], ACT.Copy,
                                                scale=consts["cw"][:, o, 0:1])
                last.then_inc(tap_done, 1)

            def exponent(w, s):
                act.wait_ge(sub_done[s], w + 1)
                nc.scalar.activation(probs[s][:], probs[s][:], ACT.Exp).then_inc(exp_done[s], 1)

            def copy_pT(w, s):
                for g in range(2):
                    act.wait_ge(pt_mm, 4 * w + 2 * s + g + 1)
                    if g == 0:
                        need(act, o_mm[s], w)
                    nc.scalar.copy(probsT[s][:, 4 * g:4 * g + 4, :],
                                   ps_pt.rearrange("p (j q) -> p j q", j=4)).then_inc(pt_sb, 1)

            def body(i, p):
                u, c, w = stage(i, 0, UNITS), stage(i, 1, UNITS), stage(i, 2, UNITS)
                if u is not None:
                    copy_xT(u, p)
                if c is not None:
                    tap(c, 1 - p, 0)
                    tap(c, 1 - p, 1)
                if w is not None:
                    exponent(w, 0)
                if c is not None:
                    tap(c, 1 - p, 2)
                if w is not None:
                    copy_pT(w, 0)
                    exponent(w, 1)
                if c is not None:
                    tap(c, 1 - p, 3)
                if w is not None:
                    copy_pT(w, 1)
                if u is not None:
                    copy_qk(u, p)

            skewed(act, UNITS, 2, body)

        @block.vector
        def _(dve):
            dve.wait_ge(zeroed, 4)

            def add_taps(u, p, g, t, ready, done):
                dve.wait_ge(ready, 4 * u + g + 1)
                for o in range(4 * g, 4 * g + 4):
                    last = nc.vector.scalar_tensor_tensor(
                        out=kc[p][:, :, o, :], in0=kpad[p][:, :, t:t + S], scalar=consts["cw"][:, o, t:t + 1],
                        in1=kc[p][:, :, o, :], op0=ALU.mult, op1=ALU.add)
                last.then_inc(done, 1)

            def row_top(w, s):
                dve.wait_ge(s_mm[s], w + 1)
                nc.vector.tensor_reduce(top[s][:], ps_s[s].rearrange("p n (h k) -> p (n h) k", k=S), AX.X,
                                        ALU.max).then_inc(top_done[s], 1)

            def subtract_top(w, s):
                dve.wait_ge(top_done[s], w + 1)
                nc.vector.tensor_tensor(topb[s][:], top[s][:], consts["cb"][:], ALU.add).then_inc(topb_done[s], 1)
                dve.wait_ge(topb_done[s], w + 1)
                nc.vector.tensor_tensor(shift[s][:], consts["cb"][:], topb[s][:],
                                        ALU.subtract).then_inc(shift_done[s], 1)
                dve.wait_ge(shift_done[s], w + 1)
                need(dve, pt_mm, 4 * w - 2 + 2 * s if isinstance(w, int) else 4 * w)
                nc.vector.tensor_tensor(probs[s][:], ps_s[s].rearrange("p n (h k) -> p (n h) k", k=S),
                                        shift[s][:].unsqueeze(2).to_broadcast([P, H, S]),
                                        ALU.add).then_inc(sub_done[s], 1)

            def normalise(w, s):
                dve.wait_ge(o_mm[s], w + 1)
                nc.vector.reciprocal(rsum[s][:], ps_vo[:, 256:512]).then_inc(rsum_done[s], 1)
                dve.wait_ge(rsum_done[s], w + 1)
                need(dve, a_mm[s], w)
                nc.vector.tensor_tensor(outT[s][:].rearrange("p n q -> p (n q)"), ps_vo[:, 0:256], rsum[s][:],
                                        ALU.mult).then_inc(o_sb[s], 1)

            def layernorm_stats(w):
                dve.wait_ge(a_mm[1], w + 1)
                dve.wait_ge(a_mm[0], w + 1)
                dve.wait_ge(xb_done, w + 1)
                nc.vector.tensor_tensor(res[:], ps_a, x_all[:, bass.ds(2 * w, 2), :], ALU.add).then_inc(res_done, 1)
                dve.wait_ge(res_done, w + 1)
                for s in range(2):
                    last = nc.vector.bn_stats(stats[:, s, :], res[:, s, :])
                dve.drain()
                for s in range(2):
                    last = nc.vector.bn_aggr(mv[:, s, :], stats[:, s, :])
                last.then_inc(mv_done, 1)

            def layernorm_apply(w):
                dve.wait_ge(rstd_done, w + 1)
                for s in range(2):
                    last = nc.vector.tensor_scalar(x_all[:, bass.ds(2 * w + s, 1), :].rearrange("p a e -> p (a e)"),
                                                   res[:, s, :], mv[:, s, 0:1],
                                                   rstd[:, s:s + 1], ALU.subtract, ALU.mult)
                last.then_inc(x1_done, 1)

            def v_block_diagonal(u, p):
                dve.wait_ge(v_mm, u + 1)
                need(dve, o_mm[1], u - 1)
                for h in range(2):
                    q = slice(64 * h, 64 * h + 64)
                    last = nc.vector.tensor_tensor(
                        vbd[p][q, :, :, h, :],
                        ps_vo.rearrange("p (b j h d) -> p j b h d", b=NB, h=2, d=DH)[q, :, :, h, :],
                        consts["bv"].rearrange("p (j h d) -> p j h d", h=2, d=DH)[q, :, h, :]
                        .unsqueeze(2).to_broadcast([64, PAIRS, NB, DH]), ALU.add)
                last.then_inc(v_sb, 1)

            def body(i, p):
                u, c, w = stage(i, 0, UNITS), stage(i, 1, UNITS), stage(i, 2, UNITS)

                def mid(g):
                    if c is not None:
                        add_taps(c, 1 - p, g, 1, tap_done, mid_done)

                def fin(g):
                    if c is not None:
                        add_taps(c, 1 - p, g, 2, mid_done, conv_done)

                if w is not None:
                    row_top(w, 0)
                mid(0)
                if w is not None:
                    subtract_top(w, 0)
                    row_top(w, 1)
                mid(1)
                fin(0)
                if w is not None:
                    subtract_top(w, 1)
                mid(2)
                fin(1)
                if w is not None:
                    normalise(w, 0)
                fin(2)
                mid(3)
                if w is not None:
                    normalise(w, 1)
                fin(3)
                if w is not None:
                    layernorm_stats(w)
                if u is not None:
                    v_block_diagonal(u, p)
                if w is not None:
                    layernorm_apply(w)

            skewed(dve, UNITS, 2, body)


def prepare(nc, ps, consts, dram, w1T, w3T, w2T):
    with ExitStack() as ctx:
        def tile(name, shape, dt=F32):
            return ctx.enter_context(nc.sbuf_tensor(name, shape, dt))

        def sem(name):
            return ctx.enter_context(nc.semaphore("p_" + name))

        natural = tile("attn_natural", [P, 4, D])
        gate_w = tile("gate_natural", [E, D])
        wo_wide = tile("wo_wide", [P, BT, 2, 4, BT, 2 * DH])
        bqs = tile("biases_q", [P, 2])
        staged = [tile(f"staged{m}", [P, 4, P]) for m in range(3)]

        small = sem("small")
        taps_w = sem("taps_w")
        attn_w = sem("attn_w")
        cross_w = sem("cross_w")
        zero, identity_made, wide_made = sem("zero"), sem("identity"), sem("wide")
        ready = consts["ready"]
        turned, copied = sem("turned"), sem("copied")
        wide_turned = sem("wide_turned")
        landed = [sem(f"landed{m}") for m in range(3)]
        w_turned = [sem(f"w_turned{m}") for m in range(3)]
        w_copied = [sem(f"w_copied{m}") for m in range(3)]

        block = ctx.enter_context(nc.Block())

        def row(ap):
            return ap.unsqueeze(0).to_broadcast([P] + list(ap.shape))

        def column(ap):
            return ap.unsqueeze(1)

        @block.sync
        def _(sp):
            for n, name in enumerate(("Wq", "Wk", "Wv", "Wo")):
                sp.dma_start(natural[:, n, :], dram["L0_attn_" + name]).then_inc(attn_w, 16)
            sp.dma_start(gate_w[:], dram["L0_ffn_gate_w"]).then_inc(attn_w, 16)
            for name, to in (("Wq", "xwq"), ("Wk", "xwk"), ("Wv", "xwv")):
                sp.dma_start(consts[to][:], dram["L0_xattn_" + name]).then_inc(cross_w, 16)
            sources = [dram["L0_ffn_w1"].rearrange("e (c f) h -> f e c h", c=4),
                       dram["L0_ffn_w3"].rearrange("e (c f) h -> f e c h", c=4),
                       dram["L0_ffn_w2"].rearrange("e h (c f) -> h e c f", c=4)]

            with sp.Fori(0, E) as e:
                for m in range(3):
                    sp.wait_ge(landed[m], 16 * e)
                    sp.wait_ge(w_turned[m], e)
                    sp.dma_start(staged[m][:], sources[m][:, bass.ds(e, 1), :, :].rearrange("p a c h -> p (a c) h")
                                 ).then_inc(landed[m], 16)
            sp.wait_ge(cross_w, 48)

        @block.scalar
        def _(act):
            for name, to in (("L0_attn_bo", "bo"), ("L0_attn_bv", "bv"), ("L0_xattn_bv", "xbv")):
                act.dma_start(consts[to], row(dram[name])).then_inc(small, 16)
            act.dma_start(bqs[:, 0:1], column(dram["L0_attn_bq"])).then_inc(small, 16)
            act.dma_start(bqs[:, 1:2], column(dram["L0_xattn_bq"])).then_inc(small, 16)
            act.dma_start(consts["bk"], column(dram["L0_attn_bk"])).then_inc(small, 16)
            act.dma_start(consts["xbk"], column(dram["L0_xattn_bk"])).then_inc(small, 16)
            act.dma_start(consts["cb"], row(dram["L0_attn_conv_b"])).then_inc(small, 16)
            act.wait_ge(small, 8 * 16)
            act.wait_ge(taps_w, H * 16)
            nc.scalar.mul(consts["bq"], bqs[:, 0:1], 1.0 / float(np.sqrt(np.float32(DH))))
            nc.scalar.mul(consts["xbq"], bqs[:, 1:2], 1.0 / float(np.sqrt(np.float32(D)))).then_inc(ready, 1)
            act.wait_ge(turned, 5)
            for n, to in enumerate(("wqT", "wkT", "wvT")):
                nc.scalar.copy(consts[to][:], ps[:, n, 0:P])
            nc.scalar.copy(consts["gateT"][:], ps[:, 3, 0:E]).then_inc(copied, 1)
            act.wait_ge(wide_turned, 1)
            nc.scalar.copy(consts["woP"][:].rearrange("p b n e -> p (b n e)"), ps[:, 4, :]).then_inc(copied, 1)
            with act.Fori(0, E) as e:
                for m, to in enumerate((w1T, w3T, w2T)):
                    act.wait_ge(w_turned[m], e + 1)
                    nc.scalar.copy(to[:, bass.ds(e * F, F)], ps[:, 5 + m, :]).then_inc(w_copied[m], 1)

        @block.gpsimd
        def _(pool):
            for i in range(H):
                pool.dma_start(consts["cw"][DH * i:DH * i + DH, :, :],
                               dram["L0_attn_conv_w"][:, i, :].unsqueeze(0).to_broadcast([DH, H, KS])
                               ).then_inc(taps_w, 16)
            nc.gpsimd.memset(consts["ident"][:], 0.0).then_inc(zero, 1)
            nc.gpsimd.memset(consts["mhalf"][:], -0.5)
            nc.gpsimd.memset(consts["eps"][:], EPS)
            nc.gpsimd.memset(wo_wide[:], 0.0).then_inc(zero, 1)
            pool.wait_ge(zero, 2)
            nc.gpsimd.affine_select(out=consts["ident"][:], in_=consts["ident"][:], compare_op=ALU.not_equal,
                                    fill=1.0, base=0, pattern=[[-1, P]], channel_multiplier=1
                                    ).then_inc(identity_made, 1)
            pool.wait_ge(attn_w, 80)
            for b in range(BT):
                last = nc.gpsimd.tensor_copy(
                    wo_wide[:, b, :, :, b, :],
                    natural[:, 3, :].rearrange("p (n j c) -> p n j c", n=2, j=4))
            last.then_inc(wide_made, 1)

        @block.vector
        def _(dve):
            for h in range(2):
                for g in range(2):
                    last = nc.vector.memset(consts["pair_ones"][64 * h:64 * h + 64, :, g, :], float(h == g))
            last.then_inc(ready, 1)

        @block.tensor
        def _(pe):
            ident = consts["ident"]
            pe.wait_ge(identity_made, 1)
            pe.wait_ge(attn_w, 80)
            for n in range(3):
                nc.tensor.transpose(ps[:, n, 0:P], natural[:, n, :], ident[:]).then_inc(turned, 1)
            nc.tensor.transpose(ps[:, 3, 0:E], gate_w[:], ident[0:E, 0:E]).then_inc(turned, 2)
            pe.wait_ge(wide_made, 1)
            for b in range(BT):
                for n in range(2):
                    last = nc.tensor.transpose(ps[:, 4, (2 * b + n) * P:(2 * b + n + 1) * P],
                                               wo_wide[:, b, n, :, :, :], ident[:])
            last.then_inc(wide_turned, 1)
            with pe.Fori(0, E) as e:
                for m in range(3):
                    pe.wait_ge(landed[m], 16 * e + 16)
                    pe.wait_ge(w_copied[m], e)
                    for c in range(4):
                        last = nc.tensor.transpose(ps[:, 5 + m, c * P:(c + 1) * P], staged[m][:, c, :], ident[:])
                    last.then_inc(w_turned[m], 1)


def cross_attention(nc, ps, consts, dram, x_all, x2T_all, gates):
    TG = 4
    UNITS = T // TG
    PR = TG // 2
    W = TG * P
    LAG = 4
    scale = 1.0 / float(np.sqrt(np.float32(D)))

    with ExitStack() as ctx:
        def tile(name, shape, dt=F32):
            return ctx.enter_context(nc.sbuf_tensor(name, shape, dt))

        def sem(name):
            return ctx.enter_context(nc.semaphore("x" + name))

        x1 = [tile(f"x1_{p}", [P, TG, D]) for p in range(2)]
        cin = [tile(f"ctx_in{p}", [P, TG, D]) for p in range(2)]
        x1T = [tile(f"x1T{p}", [P, W]) for p in range(2)]
        cT = [tile(f"ctxT{p}", [P, W]) for p in range(2)]
        qT = [tile(f"xqT{p}", [P, W]) for p in range(2)]
        kT = [tile(f"xkT{p}", [P, W]) for p in range(2)]
        v = [tile(f"xv{p}", [P, PR, BT, D]) for p in range(2)]
        probs = [tile(f"xprobs{p}", [P, TG, S]) for p in range(2)]
        weights = [tile(f"xweights{p}", [P, TG, S]) for p in range(2)]
        probsT = tile("xprobsT", [P, PR, P])
        top = tile("xtop", [P, TG])
        total = tile("xtotal", [P, TG])
        inverse = tile("xinverse", [P, TG])
        res = tile("xres", [P, TG, D])
        stats = tile("xstats", [P, TG, 6])
        mv = tile("xmv", [P, TG, 2])
        veps = tile("xveps", [P, TG])
        rstd = tile("xrstd", [P, TG])
        x2 = [tile(f"x2_{p}", [P, TG, D]) for p in range(2)]
        x2T = tile("x2T", [P, W])

        ps_xt, ps_ct, ps_q, ps_k, ps_v = (ps[:, n, :] for n in range(5))
        ps_s = ps[:, 5, 0:256].rearrange("p (t k) -> p t k", t=TG)
        ps_g = ps[:, 5, 448:480].rearrange("p (t e) -> p t e", t=TG)
        ps_o = ps[:, 6:8, 0:256].rearrange("p h (r e) -> p r h e", r=PR)
        ps_pt = ps[:, 6, 256:512].rearrange("p (r q) -> p r q", r=PR)

        ctx_landed = [sem(f"ctx_landed{p}") for p in range(2)]
        x1_done = sem("x1_done")
        xt_mm, x1T_sb, ct_mm, cT_sb = sem("xt_mm"), sem("x1T_sb"), sem("ct_mm"), sem("cT_sb")
        q_mm, q_sb, k_mm, k_sb, v_mm, v_sb = (sem(n) for n in ("q_mm", "q_sb", "k_mm", "k_sb", "v_mm", "v_sb"))
        s_mm, top_done, sub_done, exp_done = (sem(n) for n in ("s_mm", "top_done", "sub_done", "exp_done"))
        total_done, inverse_done, weights_done = (sem(n) for n in ("total_done", "inverse_done", "weights_done"))
        pt_mm, pt_sb, o_mm, res_done = (sem(n) for n in ("pt_mm", "pt_sb", "o_mm", "res_done"))
        mv_done, veps_done, rstd_done = (sem(n) for n in ("mv_done", "veps_done", "rstd_done"))
        x2_done, x2t_mm, x2T_sb, x2T_kept, gate_mm, gate_sb = (
            sem(n) for n in ("x2_done", "x2t_mm", "x2T_sb", "x2T_kept", "gate_mm", "gate_sb"))
        x2_kept = sem("x2_kept")

        ctx_tiles = dram["ctx_1024"].rearrange("(t b) s e -> (b s) t e", b=BT)
        block = ctx.enter_context(nc.Block())

        @block.sync
        def _(sp):
            def load(u, p):
                need(sp, ct_mm, u - 1)
                sp.dma_start(cin[p][:], ctx_tiles[:, bass.ds(TG * u, TG), :]).then_inc(ctx_landed[p], 16)

            for p in range(2):
                load(p, p)
            with sp.Fori(1, UNITS // 2) as two:
                for p in range(2):
                    load(2 * two + p, p)

        @block.gpsimd
        def _(pool):
            def fetch_x1(u, p):
                need(pool, xt_mm, u - 1)
                nc.gpsimd.tensor_copy(x1[p][:], x_all[:, bass.ds(TG * u, TG), :]).then_inc(x1_done, 1)

            def rsqrt(w):
                pool.wait_ge(mv_done, w + 1)
                nc.gpsimd.tensor_tensor(veps[:], mv[:, :, 1], consts["eps"][:, 0:mv.shape[1]], ALU.add).then_inc(veps_done, 1)
                pool.wait_ge(veps_done, w + 1)
                nc.gpsimd.tensor_tensor(rstd[:], veps[:], consts["mhalf"][:, 0:TG], ALU.pow).then_inc(rstd_done, 1)

            def keep_x2(w, p):
                pool.wait_ge(x2_done, w + 1)
                nc.gpsimd.tensor_copy(x_all[:, bass.ds(TG * w, TG), :], x2[p][:]).then_inc(x2_kept, 1)

            def body(i, p):
                if (u := stage(i, 0, UNITS)) is not None:
                    fetch_x1(u, p)
                if (w := stage(i, 3, UNITS)) is not None:
                    rsqrt(w)
                    keep_x2(w, 1 - p)

            skewed(pool, UNITS, LAG, body)

        @block.tensor
        def _(pe):
            ident = consts["ident"]

            def x_transposes(u, p):
                pe.wait_ge(x1_done, u + 1)
                need(pe, x1T_sb, u)
                for t in range(TG):
                    last = nc.tensor.transpose(ps_xt[:, t * P:(t + 1) * P], x1[p][:, t, :], ident[:])
                last.then_inc(xt_mm, 1)

            def ctx_transposes(u, p):
                pe.wait_ge(ctx_landed[p], 8 * (u - p) + 16)
                need(pe, cT_sb, u)
                need(pe, x2T_sb, u - 4)
                for t in range(TG):
                    last = nc.tensor.transpose(ps_ct[:, t * P:(t + 1) * P], cin[p][:, t, :], ident[:])
                last.then_inc(ct_mm, 1)

            def products(u, p):
                pe.wait_ge(x1T_sb, u + 1)
                need(pe, q_sb, u)
                nc.tensor.matmul(ps_q, consts["xwq"][:], x1T[p][:], start=True, stop=True).then_inc(q_mm, 1)
                pe.wait_ge(cT_sb, u + 1)
                need(pe, k_sb, u)
                nc.tensor.matmul(ps_k, consts["xwk"][:], cT[p][:], start=True, stop=True).then_inc(k_mm, 1)
                need(pe, v_sb, u)
                for r in range(PR):
                    for b in range(BT):
                        for h in range(2):
                            c = (2 * r + h) * P + b * S
                            last = nc.tensor.matmul(ps_v[64 * h:64 * h + 64, (BT * r + b) * D:(BT * r + b + 1) * D],
                                                    cT[p][:, c:c + S], consts["xwv"][:], start=True, stop=True)
                last.then_inc(v_mm, 1)

            def scores(w, p):
                pe.wait_ge(q_sb, w + 1)
                pe.wait_ge(k_sb, w + 1)
                need(pe, sub_done, w)
                need(pe, gate_sb, w - 2)
                for t in range(TG):
                    for b in range(BT):
                        c = slice(t * P + b * S, t * P + (b + 1) * S)
                        last = nc.tensor.matmul(ps_s[64 * b:64 * b + 64, t, :], qT[p][:, c], kT[p][:, c],
                                                start=True, stop=True)
                last.then_inc(s_mm, 1)

            def p_transposes(w, p):
                pe.wait_ge(weights_done, w + 1)
                need(pe, pt_sb, w)
                need(pe, res_done, w)
                for r in range(PR):
                    last = nc.tensor.transpose(ps_pt[:, r, :], weights[p][:, 2 * r:2 * r + 2, :], ident[:])
                last.then_inc(pt_mm, 1)

            def outputs_ready(w):
                pe.wait_ge(pt_sb, w + 1)
                pe.wait_ge(v_sb, w + 1)

            def outputs(w, p):
                for r in range(PR):
                    for b in range(BT):
                        for h in range(2):
                            k = slice(64 * h, 64 * h + 64)
                            last = nc.tensor.matmul(ps_o[64 * b:64 * b + 64, r, h, :],
                                                    probsT[k, r, b * S:(b + 1) * S], v[p][k, r, b, :],
                                                    start=True, stop=True)
                last.then_inc(o_mm, 1)

            def x2_transposes(w, p):
                pe.wait_ge(x2_done, w + 1)
                pe.wait_ge(cT_sb, upto(w + 5, UNITS))
                for t in range(TG):
                    last = nc.tensor.transpose(ps_ct[:, t * P:(t + 1) * P], x2[p][:, t, :], ident[:])
                last.then_inc(x2t_mm, 1)

            def gate(w):
                pe.wait_ge(x2T_sb, w + 1)
                pe.wait_ge(sub_done, upto(w + 3, UNITS))
                need(pe, gate_sb, w)
                for t in range(TG):
                    last = nc.tensor.matmul(ps_g[:, t, :], x2T[:, t * P:(t + 1) * P], consts["gateT"][:],
                                            start=True, stop=True)
                last.then_inc(gate_mm, 1)

            def body(i, p):
                if (w := stage(i, 2, UNITS)) is not None:
                    scores(w, p)
                if (u := stage(i, 0, UNITS)) is not None:
                    x_transposes(u, p)
                    ctx_transposes(u, p)
                if (w := stage(i, 3, UNITS)) is not None:
                    p_transposes(w, 1 - p)
                if (u := stage(i, 1, UNITS)) is not None:
                    products(u, 1 - p)
                if (w := stage(i, 3, UNITS)) is not None:
                    outputs_ready(w)
                if (w := stage(i, 4, UNITS)) is not None:
                    x2_transposes(w, p)
                if (w := stage(i, 3, UNITS)) is not None:
                    outputs(w, 1 - p)
                if (w := stage(i, 4, UNITS)) is not None:
                    gate(w)

            skewed(pe, UNITS, LAG, body)

        @block.scalar
        def _(act):
            def copy_xT(u, p):
                act.wait_ge(xt_mm, u + 1)
                need(act, q_mm, u - 1)
                nc.scalar.copy(x1T[p][:], ps_xt).then_inc(x1T_sb, 1)
                act.wait_ge(ct_mm, u + 1)
                need(act, v_mm, u - 1)
                nc.scalar.copy(cT[p][:], ps_ct).then_inc(cT_sb, 1)

            def copy_qk(u, p):
                act.wait_ge(q_mm, u + 1)
                need(act, s_mm, u - 1)
                nc.scalar.activation(qT[p][:], ps_q, ACT.Identity, bias=consts["xbq"][:],
                                     scale=scale).then_inc(q_sb, 1)
                act.wait_ge(k_mm, u + 1)
                nc.scalar.activation(kT[p][:], ps_k, ACT.Identity, bias=consts["xbk"][:]).then_inc(k_sb, 1)

            def exponent(w, p):
                act.wait_ge(sub_done, w + 1)
                nc.scalar.activation(probs[p][:], probs[p][:], ACT.Exp).then_inc(exp_done, 1)

            def copy_pT(w):
                act.wait_ge(pt_mm, w + 1)
                need(act, o_mm, w)
                nc.scalar.copy(probsT[:], ps_pt).then_inc(pt_sb, 1)

            def copy_x2T(w):
                act.wait_ge(x2t_mm, w + 1)
                need(act, gate_mm, w)
                need(act, x2T_kept, w)
                nc.scalar.copy(x2T[:], ps_ct).then_inc(x2T_sb, 1)
                act.wait_ge(x2T_sb, w + 1)
                nc.scalar.copy(x2T_all[:, bass.ds(w * W, W)], x2T[:]).then_inc(x2T_kept, 1)

            def body(i, p):
                if (u := stage(i, 0, UNITS)) is not None:
                    copy_xT(u, p)
                if (w := stage(i, 2, UNITS)) is not None:
                    exponent(w, p)
                if (w := stage(i, 3, UNITS)) is not None:
                    copy_pT(w)
                if (u := stage(i, 1, UNITS)) is not None:
                    copy_qk(u, 1 - p)
                if (w := stage(i, 4, UNITS)) is not None:
                    copy_x2T(w)

            skewed(act, UNITS, LAG, body)

        @block.vector
        def _(dve):
            def bias_v(u, p):
                dve.wait_ge(v_mm, u + 1)
                need(dve, o_mm, u - 1)
                nc.vector.tensor_tensor(v[p][:].rearrange("p r b e -> p (r b) e"),
                                        ps_v.rearrange("p (n e) -> p n e", e=D),
                                        consts["xbv"].unsqueeze(1).to_broadcast([P, TG, D]),
                                        ALU.add).then_inc(v_sb, 1)

            def subtract_top(w, p):
                dve.wait_ge(s_mm, w + 1)
                nc.vector.tensor_reduce(top[:], ps_s, AX.X, ALU.max).then_inc(top_done, 1)
                dve.wait_ge(top_done, w + 1)
                nc.vector.tensor_tensor(probs[p][:], ps_s, top[:].unsqueeze(2).to_broadcast([P, TG, S]),
                                        ALU.subtract).then_inc(sub_done, 1)

            def normalise(w, p):
                dve.wait_ge(exp_done, w + 1)
                nc.vector.tensor_reduce(total[:], probs[p][:], AX.X, ALU.add).then_inc(total_done, 1)
                dve.wait_ge(total_done, w + 1)
                nc.vector.reciprocal(inverse[:], total[:]).then_inc(inverse_done, 1)
                dve.wait_ge(inverse_done, w + 1)
                need(dve, pt_mm, w - 1)
                nc.vector.tensor_tensor(weights[p][:], probs[p][:],
                                        inverse[:].unsqueeze(2).to_broadcast([P, TG, S]),
                                        ALU.mult).then_inc(weights_done, 1)

            def layernorm_stats(w):
                dve.wait_ge(o_mm, w + 1)
                nc.vector.tensor_tensor(res[:].rearrange("p (r h) e -> p r h e", h=2), ps_o,
                                        x_all[:, bass.ds(w * TG, TG), :].rearrange("p (r h) e -> p r h e", h=2),
                                        ALU.add).then_inc(res_done, 1)
                dve.wait_ge(res_done, w + 1)
                for t in range(TG):
                    last = nc.vector.bn_stats(stats[:, t, :], res[:, t, :])
                dve.drain()
                for t in range(TG):
                    last = nc.vector.bn_aggr(mv[:, t, :], stats[:, t, :])
                last.then_inc(mv_done, 1)

            def layernorm_apply(w, p):
                dve.wait_ge(rstd_done, w + 1)
                need(dve, x2t_mm, w - 1)
                need(dve, x2_kept, w - 1)
                for t in range(TG):
                    last = nc.vector.tensor_scalar(x2[p][:, t, :], res[:, t, :], mv[:, t, 0:1], rstd[:, t:t + 1],
                                                   ALU.subtract, ALU.mult)
                last.then_inc(x2_done, 1)

            def copy_gate(w):
                dve.wait_ge(gate_mm, w + 1)
                nc.vector.tensor_copy(gates[:, bass.ds(w * TG, TG), :], ps_g).then_inc(gate_sb, 1)

            def body(i, p):
                if (w := stage(i, 2, UNITS)) is not None:
                    subtract_top(w, p)
                if (u := stage(i, 1, UNITS)) is not None:
                    bias_v(u, 1 - p)
                if (w := stage(i, 3, UNITS)) is not None:
                    layernorm_stats(w)
                if (w := stage(i, 2, UNITS)) is not None:
                    normalise(w, p)
                if (w := stage(i, 3, UNITS)) is not None:
                    layernorm_apply(w, 1 - p)
                if (w := stage(i, 4, UNITS)) is not None:
                    copy_gate(w)

            skewed(dve, UNITS, LAG, body)


def route(nc, consts, gates, wtok):
    with ExitStack() as ctx:
        def tile(name, shape, dt=F32):
            return ctx.enter_context(nc.sbuf_tensor("r_" + name, shape, dt))

        def sem(name):
            return ctx.enter_context(nc.semaphore("r_" + name))

        rank = tile("rank", [P, E])
        top = [tile(f"top{n}", [P, T]) for n in range(2)]
        first = tile("first", [P, T])
        total = tile("total", [P, T])
        rest = tile("rest", [P, T, E])
        size = tile("size", [P, T, E])
        gap = tile("gap", [P, T, E])
        kept = tile("kept", [P, T, E])
        ex = [tile(f"ex{n}", [P, T, E]) for n in range(2)]
        chosen = [tile(f"chosen{n}", [P, T, E]) for n in range(2)]
        step, ranks, gap_made, ex_made = sem("step"), sem("ranks"), sem("gap_made"), sem("ex_made")

        block = ctx.enter_context(nc.Block())

        @block.gpsimd
        def _(pool):
            for e in range(E):
                last = nc.gpsimd.memset(rank[:, e:e + 1], float(E - e))
            last.then_inc(ranks, 1)

        @block.scalar
        def _(act):
            for n in range(2):
                act.wait_ge(gap_made, n + 1)
                nc.scalar.activation(ex[n][:], ex[n][:], ACT.Exp).then_inc(ex_made, 1)

        @block.vector
        def _(dve):
            done = [0]

            def then(instruction):
                done[0] += 1
                instruction.then_inc(step, 1)
                dve.wait_ge(step, done[0])

            def wide(ap):
                return ap.unsqueeze(2).to_broadcast([P, T, E])

            dve.wait_ge(ranks, 1)
            s = gates[:]
            for n in range(2):
                source = s if n == 0 else rest[:]
                then(nc.vector.tensor_reduce(top[n][:], source, AX.X, ALU.max))
                then(nc.vector.tensor_tensor(chosen[n][:], source, wide(top[n][:]), ALU.is_equal))
                then(nc.vector.tensor_tensor(chosen[n][:], chosen[n][:],
                                             rank[:].unsqueeze(1).to_broadcast([P, T, E]), ALU.mult))
                then(nc.vector.tensor_reduce(first[:], chosen[n][:], AX.X, ALU.max))
                then(nc.vector.tensor_tensor(chosen[n][:], chosen[n][:], wide(first[:]), ALU.is_equal))
                if n == 0:
                    then(nc.vector.tensor_scalar(kept[:], chosen[0][:], -1.0, 1.0, ALU.mult, ALU.add))
                    then(nc.vector.tensor_tensor(rest[:], s, kept[:], ALU.mult))
                    then(nc.vector.scalar_tensor_tensor(out=rest[:], in0=chosen[0][:], scalar=-3.0e38, in1=rest[:],
                                                        op0=ALU.mult, op1=ALU.add))
                then(nc.vector.tensor_scalar(size[:], s, -1.0, None, ALU.mult))
                then(nc.vector.tensor_tensor(size[:], size[:], s, ALU.max))
                then(nc.vector.tensor_tensor(size[:], size[:], wide(top[n][:]), ALU.max))
                then(nc.vector.tensor_scalar(size[:], size[:], 2 * JITTER, None, ALU.mult))
                then(nc.vector.tensor_tensor(gap[:], wide(top[n][:]), s, ALU.subtract))
                then(nc.vector.tensor_tensor(gap[:], gap[:], size[:], ALU.is_le))
                if n == 1:
                    then(nc.vector.tensor_tensor(gap[:], gap[:], kept[:], ALU.mult))
                then(nc.vector.tensor_tensor(ex[n][:], s, wide(top[n][:]), ALU.subtract))
                nc.vector.tensor_scalar(ex[n][:], ex[n][:], 0.0, None, ALU.min).then_inc(gap_made, 1)
                dve.wait_ge(ex_made, n + 1)
                then(nc.vector.tensor_tensor(ex[n][:], ex[n][:], gap[:], ALU.mult))
                then(nc.vector.tensor_reduce(total[:], ex[n][:], AX.X, ALU.add))
                then(nc.vector.reciprocal(total[:], total[:]))
                then(nc.vector.tensor_tensor(chosen[n][:], chosen[n][:], wide(total[:]), ALU.mult))
            then(nc.vector.tensor_tensor(wtok[:], chosen[0][:], chosen[1][:], ALU.add))


def experts(nc, ps, consts, dram, x_all, x2T_all, wtok, w1T, w3T, w2T):
    TG = 4
    CHUNKS = T // TG
    W = TG * P
    FC = F // P
    STEPS = E * FC
    with ExitStack() as ctx:
        def tile(name, shape, dt=F32):
            return ctx.enter_context(nc.sbuf_tensor("f_" + name, shape, dt))

        def sem(name):
            return ctx.enter_context(nc.semaphore("f_" + name))

        silu = [tile(f"silu{n}", [P, W]) for n in range(2)]
        hidden = [tile(f"hidden{n}", [P, W]) for n in range(4)]
        acc = tile("acc", [P, TG, D])
        out = tile("out", [P, TG, D])
        stats = tile("stats", [P, TG, 6])
        mv = tile("mv", [P, TG, 2])
        veps = tile("veps", [P, TG])
        rstd = tile("rstd", [P, TG])
        h_mm, silu_done, hidden_done, y_mm = sem("h_mm"), sem("silu"), sem("hidden"), sem("y_mm")
        acc_done, mv_done = sem("acc_done"), sem("mv_done")
        veps_done, rstd_done, out_done, stored = sem("veps"), sem("rstd"), sem("out_done"), sem("stored")
        ps_1 = [ps[:, n, :] for n in range(2)]
        ps_3 = [ps[:, 2 + n, :] for n in range(2)]
        ps_y = [ps[:, 4 + n, :] for n in range(2)]
        out_tiles = dram["out"].rearrange("(t b) s e -> (b s) t e", b=BT)
        block = ctx.enter_context(nc.Block())

        @block.sync
        def _(sp):
            with sp.Fori(0, CHUNKS) as c:
                sp.wait_ge(out_done, c + 1)
                sp.dma_start(out_tiles[:, bass.ds(TG * c, TG), :], out[:]).then_inc(stored, 16)
            sp.wait_ge(stored, 16 * CHUNKS)

        @block.gpsimd
        def _(pool):
            with pool.Fori(0, CHUNKS) as c:
                pool.wait_ge(mv_done, c + 1)
                nc.gpsimd.tensor_tensor(veps[:], mv[:, :, 1], consts["eps"][:, 0:mv.shape[1]], ALU.add).then_inc(veps_done, 1)
                pool.wait_ge(veps_done, c + 1)
                nc.gpsimd.tensor_tensor(rstd[:], veps[:], consts["mhalf"][:, 0:TG], ALU.pow).then_inc(rstd_done, 1)

        @block.tensor
        def _(pe):
            def hidden_products(c, m):
                pe.wait_ge(hidden_done, STEPS * c + (m - 1 if m >= 2 else 0))
                cols = slice(m * P, (m + 1) * P)
                x = x2T_all[:, bass.ds(c * W, W)]
                nc.tensor.matmul(ps_1[m % 2], w1T[:, cols], x, start=True, stop=True)
                nc.tensor.matmul(ps_3[m % 2], w3T[:, cols], x, start=True, stop=True).then_inc(h_mm, 1)

            def output_products(c, m):
                e, f = m // FC, m % FC
                pe.wait_ge(hidden_done, STEPS * c + m + 1)
                if f == 0:
                    pe.wait_ge(acc_done, E * c + (e - 1 if e >= 2 else 0))
                for t in range(TG):
                    last = nc.tensor.matmul(ps_y[e % 2][:, t * D:(t + 1) * D], hidden[m % 4][:, t * P:(t + 1) * P],
                                            w2T[:, m * P:(m + 1) * P], start=(f == 0 and t == 0),
                                            stop=(f == FC - 1), skip_group_check=True)
                last.then_inc(y_mm, 1)

            with pe.Fori(0, CHUNKS) as c:
                for m in range(STEPS + 2):
                    if m < STEPS:
                        hidden_products(c, m)
                    if m >= 2:
                        output_products(c, m - 2)

        @block.scalar
        def _(act):
            with act.Fori(0, CHUNKS) as c:
                for m in range(STEPS):
                    act.wait_ge(h_mm, STEPS * c + m + 1)
                    act.wait_ge(hidden_done, STEPS * c + (m - 1 if m >= 2 else 0))
                    nc.scalar.activation(silu[m % 2][:], ps_1[m % 2], ACT.Silu).then_inc(silu_done, 1)

        @block.vector
        def _(dve):
            def hidden_step(c, m):
                dve.wait_ge(silu_done, STEPS * c + m + 1)
                dve.wait_ge(y_mm, STEPS * c + (m - 3 if m >= 4 else 0))
                nc.vector.tensor_tensor(hidden[m % 4][:], ps_3[m % 2], silu[m % 2][:],
                                        ALU.mult).then_inc(hidden_done, 1)

            def add_expert(c, e):
                dve.wait_ge(y_mm, STEPS * c + FC * e + FC)
                if e:
                    dve.wait_ge(acc_done, E * c + e)
                for t in range(TG):
                    old = acc[:, t, :] if e else x_all[:, bass.ds(TG * c + t, 1), :].rearrange("p a e -> p (a e)")
                    last = nc.vector.scalar_tensor_tensor(
                        out=acc[:, t, :], in0=ps_y[e % 2][:, t * D:(t + 1) * D],
                        scalar=wtok[:, bass.ds(TG * c + t, 1), e], in1=old, op0=ALU.mult, op1=ALU.add)
                last.then_inc(acc_done, 1)

            with dve.Fori(0, CHUNKS) as c:
                for m in range(STEPS):
                    hidden_step(c, m)
                    if m % FC == 3 and m > FC:
                        add_expert(c, m // FC - 1)
                add_expert(c, E - 1)
                dve.wait_ge(acc_done, E * c + E)
                for t in range(TG):
                    last = nc.vector.bn_stats(stats[:, t, :], acc[:, t, :])
                dve.drain()
                for t in range(TG):
                    last = nc.vector.bn_aggr(mv[:, t, :], stats[:, t, :])
                last.then_inc(mv_done, 1)
                dve.wait_ge(rstd_done, c + 1)
                dve.wait_ge(stored, 16 * c)
                for t in range(TG):
                    last = nc.vector.tensor_scalar(out[:, t, :], acc[:, t, :], mv[:, t, 0:1], rstd[:, t:t + 1],
                                                   ALU.subtract, ALU.mult)
                last.then_inc(out_done, 1)


def decoder(nc, dram):
    with ExitStack() as ctx:
        def tile(name, shape, dt=F32):
            return ctx.enter_context(nc.sbuf_tensor(name, shape, dt))

        x_all = tile("x_all", [P, T, D])
        ps = ctx.enter_context(nc.psum_tensor("ps", [P, 8, 512], F32))
        w1T, w3T, w2T = (tile(n, [P, E * F]) for n in ("w1T", "w3T", "w2T"))
        shapes = {"ident": [P, P], "bo": [P, D], "bv": [P, D], "xbv": [P, D], "bq": [P, 1], "xbq": [P, 1],
                  "bk": [P, 1], "xbk": [P, 1], "cb": [P, H], "cw": [P, H, KS], "wqT": [P, P], "wkT": [P, P],
                  "wvT": [P, P], "woP": [P, BT, 2, D], "pair_ones": [P, BT, 2, DH], "mhalf": [P, 4], "eps": [P, 4],
                  "xwq": [P, P], "xwk": [P, P], "xwv": [P, P], "gateT": [P, E]}
        consts = {n: tile("c_" + n, shape)[:] for n, shape in shapes.items()}
        consts["ready"] = ctx.enter_context(nc.semaphore("constants_ready"))
        prepare(nc, ps, consts, dram, w1T, w3T, w2T)
        self_attention(nc, tile, ps, consts, dram, x_all)
        x2T_all = tile("x2T_all", [P, T * P])
        gates = tile("gates", [P, T, E])
        wtok = tile("wtok", [P, T, E])
        cross_attention(nc, ps, consts, dram, x_all, x2T_all, gates)
        route(nc, consts, gates, wtok)
        experts(nc, ps, consts, dram, x_all, x2T_all, wtok, w1T, w3T, w2T)


_INS = ["x", "ctx_1024", "L0_attn_Wq", "L0_attn_bq", "L0_attn_Wk", "L0_attn_bk", "L0_attn_Wv", "L0_attn_bv",
        "L0_attn_Wo", "L0_attn_bo", "L0_attn_conv_w", "L0_attn_conv_b", "L0_xattn_Wq", "L0_xattn_bq",
        "L0_xattn_Wk", "L0_xattn_bk", "L0_xattn_Wv", "L0_xattn_bv", "L0_ffn_gate_w", "L0_ffn_w1", "L0_ffn_w2",
        "L0_ffn_w3"]


def kernel(**inputs):
    import concourse.bacc as bacc
    from concourse.bass_utils import run_bass_kernel_spmd

    nc = bacc.Bacc("TRN2", target_bir_lowering=False, num_devices=1)
    arrays, dram = {}, {}
    for name in _INS:
        a = np.ascontiguousarray(inputs[name])
        arrays[f"in_{name}"] = a
        dram[name] = nc.dram_tensor(f"in_{name}", a.shape, mybir.dt.from_np(a.dtype), kind="ExternalInput").ap()
    dram["out"] = nc.dram_tensor("out_0", (B, S, D), F32, kind="ExternalOutput").ap()
    decoder(nc, dram)
    result = run_bass_kernel_spmd(nc, [arrays], core_ids=[0])
    return result.results[0]["out_0"]
```

```python
from contextlib import ExitStack

import numpy as np

import concourse.bass as bass
from concourse import mybir

F32 = mybir.dt.float32
U32 = mybir.dt.uint32
I32 = mybir.dt.int32
BF16 = mybir.dt.bfloat16
ALU = mybir.AluOpType
ACT = mybir.ActivationFunctionType
AX = mybir.AxisListType

B, S, D = 128, 64, 128
H, DH, KS = 16, 8, 3
E, F = 8, 512
TOP = 2
WT = 512
ROWS = B * S + WT
NT = TOP * B * S // WT + E - 1
RW = D + 2
P = 128
T = B * S // P
BT = P // S
PAIRS = H // 2
EPS = 1e-5
JITTER = 0.01


def need(engine, semaphore, value):
    if not (isinstance(value, int) and value <= 0):
        engine.wait_ge(semaphore, value)


def skewed(engine, units, lag, start, body, ahead=0):
    end = (units - ahead) // 2 * 2
    for i in range(start):
        body(i, i % 2)
    with engine.Fori(start // 2, end // 2) as two:
        for p in range(2):
            body(2 * two + p, p)
    for i in range(end, units + lag):
        body(i, i % 2)


def upto(count, units):
    return min(count, units) if isinstance(count, int) else count


def stage(i, lag, units):
    u = i - lag
    if isinstance(i, int) and not 0 <= u < units:
        return None
    return u


def self_attention(nc, ps, consts, dram, x_all):
    UNITS = T // 2
    NB = 2 * BT
    LAG, START = 3, 4
    scale = 1.0 / float(np.sqrt(np.float32(DH)))

    with ExitStack() as ctx:
        def tile(name, shape, dt=F32):
            return ctx.enter_context(nc.sbuf_tensor(name, shape, dt))

        def sem(name):
            return ctx.enter_context(nc.semaphore(name))

        x_in = [tile(f"x_in{p}", [P, 2, D]) for p in range(2)]
        xT = [tile(f"xT{p}", [P, 2 * P]) for p in range(2)]
        qT = [tile(f"qT{p}", [P, 2 * P]) for p in range(2)]
        kpad = [tile(f"kpad{p}", [P, NB, S + 2]) for p in range(2)]
        kc = [tile(f"kc{p}", [P, NB, H, S]) for p in range(2)]
        kc3 = [tile(f"kc3_{p}", [P, NB, H // 2, S]) for p in range(2)]
        vbd = [tile(f"vbd{p}", [P, PAIRS, NB, 2, DH]) for p in range(2)]
        probs = [tile(f"probs{s}", [P, H, S]) for s in range(2)]
        probsT = [tile(f"probsT{s}", [P, PAIRS, P]) for s in range(2)]
        total = [tile(f"total{s}", [P, H]) for s in range(2)]
        inverse = [tile(f"inverse{s}", [P, H]) for s in range(2)]
        outT = [tile(f"outT{s}", [P, 2, P]) for s in range(2)]
        top = [tile(f"top{s}", [P, H]) for s in range(2)]
        topb = [tile(f"topb{s}", [P, H]) for s in range(2)]
        shift = [tile(f"shift{s}", [P, H]) for s in range(2)]
        res = tile("res", [P, 2, D])
        stats = tile("stats", [P, 2, 6])
        mv = tile("mv", [P, 2, 2])
        veps = tile("veps", [P, 2])
        rstd = tile("rstd", [P, 2])

        ps_s = [ps[:, 2 * s:2 * s + 2, :] for s in range(2)]
        ps_pt = ps[:, 4, :]
        ps_qk = ps[:, 5, :]
        ps_vo = ps[:, 6, :]
        ps_x = ps[:, 7, 0:256]
        ps_a = ps[:, 7, 256:512].rearrange("p (s e) -> p s e", s=2)

        x_landed = [sem(f"x_landed{p}") for p in range(2)]
        xb_done = sem("xb_done")
        xT_mm, xT_sb = sem("xT_mm"), sem("xT_sb")
        qk_mm, q_sb, k_sb = sem("qk_mm"), sem("q_sb"), sem("k_sb")
        v_mm, v_sb = sem("v_mm"), sem("v_sb")
        tap_done, mid_done, conv_done = sem("tap_done"), sem("mid_done"), sem("conv_done")
        s_mm = [sem(f"s_mm{s}") for s in range(2)]
        top_done = [sem(f"top_done{s}") for s in range(2)]
        topb_done = [sem(f"topb_done{s}") for s in range(2)]
        shift_done = [sem(f"shift_done{s}") for s in range(2)]
        inverse_done = [sem(f"inverse_done{s}") for s in range(2)]
        norm_done = [sem(f"norm_done{s}") for s in range(2)]
        exp_done = [sem(f"exp_done{s}") for s in range(2)]
        pt_mm, pt_sb = sem("pt_mm"), sem("pt_sb")
        o_mm = [sem(f"o_mm{s}") for s in range(2)]
        o_sb = [sem(f"o_sb{s}") for s in range(2)]
        a_mm = [sem(f"a_mm{s}") for s in range(2)]
        res_done, mv_done = sem("res_done"), sem("mv_done")
        veps_done, rstd_done, x1_done = sem("veps_done"), sem("rstd_done"), sem("x1_done")
        zeroed, pool_taps, pool_conv = sem("zeroed"), sem("pool_taps"), sem("pool_conv")

        x_tiles = dram["x"].rearrange("(t b) s e -> (b s) t e", b=BT)
        block = ctx.enter_context(nc.Block())

        @block.sync
        def _(sp):
            def load(u, p):
                need(sp, xT_mm, u - 1)
                need(sp, xb_done, u - 1)
                sp.dma_start(x_in[p][:], x_tiles[:, bass.ds(2 * u, 2), :]).then_inc(x_landed[p], 16)

            for u in range(4):
                load(u, u % 2)
            with sp.Fori(2, UNITS // 2) as two:
                for p in range(2):
                    load(2 * two + p, p)

        @block.gpsimd
        def _(pool):
            for p in range(2):
                nc.gpsimd.memset(kpad[p][:], 0.0).then_inc(zeroed, 1)
                nc.gpsimd.memset(vbd[p][:], 0.0).then_inc(zeroed, 1)

            def residual_in(u, p):
                pool.wait_ge(x_landed[p], 8 * (u - p) + 16)
                nc.gpsimd.tensor_tensor(x_all[:, bass.ds(2 * u, 2), :], x_in[p][:],
                                        consts["bo"].unsqueeze(1).to_broadcast([P, 2, D]),
                                        ALU.add).then_inc(xb_done, 1)

            def rsqrt(w):
                pool.wait_ge(mv_done, w + 1)
                nc.gpsimd.tensor_tensor(veps[:], mv[:, :, 1], consts["eps"][:, 0:2], ALU.add)
                pool.drain()
                nc.gpsimd.tensor_tensor(rstd[:], veps[:], consts["mhalf"][:, 0:2], ALU.pow).then_inc(rstd_done, 1)

            def normalise(w, s):
                pool.wait_ge(inverse_done[s], w + 1)
                nc.gpsimd.tensor_tensor(probs[s][:], probs[s][:],
                                        inverse[s][:].unsqueeze(2).to_broadcast([P, H, S]),
                                        ALU.mult).then_inc(norm_done[s], 1)

            def tap(c, p, g, t, to, done):
                nc.gpsimd.tensor_tensor(
                    to, kpad[p][:, :, t:t + S].unsqueeze(2).to_broadcast([P, NB, 4, S]),
                    consts["cw"][:, 4 * g:4 * g + 4, t].unsqueeze(1).unsqueeze(3).to_broadcast([P, NB, 4, S]),
                    ALU.mult).then_inc(done, 1)

            def conv(c, p):
                pool.wait_ge(k_sb, c + 1)
                need(pool, s_mm[1], c - 1)
                for g in (2, 3):
                    tap(c, p, g, 0, kc[p][:, :, 4 * g:4 * g + 4, :], pool_taps)
                for g in (2, 3):
                    tap(c, p, g, 2, kc3[p][:, :, 4 * g - 8:4 * g - 4, :], pool_conv)

            def body(i, p):
                u, c, w, z = stage(i, 0, UNITS), stage(i, 1, UNITS), stage(i, 2, UNITS), stage(i, 3, UNITS)
                if c is not None:
                    conv(c, 1 - p)
                if u is not None:
                    residual_in(u, p)
                if w is not None:
                    normalise(w, 0)
                if z is not None:
                    rsqrt(z)
                if w is not None:
                    normalise(w, 1)

            skewed(pool, UNITS, LAG, START, body)

        @block.tensor
        def _(pe):
            ident = consts["ident"]

            def x_transposes(u, p):
                pe.wait_ge(x_landed[p], 8 * (u - p) + 16)
                need(pe, xT_sb, u)
                need(pe, res_done, u - 3)
                for s in range(2):
                    last = nc.tensor.transpose(ps_x[:, s * P:(s + 1) * P], x_in[p][:, s, :], ident[:])
                last.then_inc(xT_mm, 1)

            def qk_products(u, p):
                pe.wait_ge(xT_sb, u + 1)
                need(pe, k_sb, u)
                nc.tensor.matmul(ps_qk[:, 0:256], consts["wqT"][:], xT[p][:], start=True, stop=True)
                nc.tensor.matmul(ps_qk[:, 256:512], consts["wkT"][:], xT[p][:],
                                 start=True, stop=True).then_inc(qk_mm, 1)

            def v_products(u, p):
                need(pe, v_sb, u)
                need(pe, o_sb[1], u - 1)
                for b in range(NB):
                    for h in range(2):
                        last = nc.tensor.matmul(ps_vo[64 * h:64 * h + 64, b * D:(b + 1) * D],
                                                xT[p][:, b * S:(b + 1) * S], consts["wvT"][:],
                                                start=True, stop=True)
                last.then_inc(v_mm, 1)

            def scores(w, p, s):
                if s == 0:
                    pe.wait_ge(q_sb, w + 1)
                    pe.wait_ge(conv_done, 4 * w + 4)
                    pe.wait_ge(pool_conv, 2 * w + 2)
                need(pe, exp_done[s], w)
                for half in range(2):
                    for b in range(BT):
                        keys = [kc[p][:, BT * s + b, 8 * half:8 * half + 8, :], kc3[p][:, BT * s + b, :, :]]
                        for n in range(half + 1):
                            last = nc.tensor.matmul(
                                ps_s[s][64 * b:64 * b + 64, half, :],
                                qT[p][:, s * P + b * S:s * P + (b + 1) * S],
                                keys[n], start=(n == 0), stop=(n == half))
                last.then_inc(s_mm[s], 1)

            def p_transposes(w, s):
                pe.wait_ge(norm_done[s], w + 1)
                for g in range(2):
                    need(pe, pt_sb, 4 * w + 2 * s + g)
                    for j in range(4):
                        last = nc.tensor.transpose(ps_pt[:, j * P:(j + 1) * P],
                                                   probs[s][:, 8 * g + 2 * j:8 * g + 2 * j + 2, :], ident[:])
                    last.then_inc(pt_mm, 1)

            def outputs(w, p, s):
                pe.wait_ge(pt_sb, 4 * w + 2 * s + 2)
                if s == 0:
                    pe.wait_ge(v_sb, upto(w + 2, UNITS))
                else:
                    pe.wait_ge(o_sb[0], w + 1)
                for j in range(PAIRS):
                    q = slice(32 * (j % 4), 32 * (j % 4) + 32)
                    c = (j // 4) * P
                    last = nc.tensor.matmul(ps_vo[q, c:c + P], vbd[p][:, j, BT * s:BT * s + BT, :, :],
                                            probsT[s][:, j, :], start=True, stop=True,
                                            tile_position=(0, 32 * (j % 4)))
                last.then_inc(o_mm[s], 1)

            def projection(w, s):
                pe.wait_ge(o_sb[s], w + 1)
                pe.wait_ge(xT_sb, upto(w + 4, UNITS))
                for half in range(2):
                    for b in range(BT):
                        last = nc.tensor.matmul(ps_a[64 * b:64 * b + 64, s, :],
                                                outT[s][:, half, b * S:(b + 1) * S],
                                                consts["woP"][:, b, half, :],
                                                start=(half == 0), stop=(half == 1))
                last.then_inc(a_mm[s], 1)

            def body(i, p):
                u, c, w, z = stage(i, 0, UNITS), stage(i, 1, UNITS), stage(i, 2, UNITS), stage(i, 3, UNITS)
                if w is not None:
                    scores(w, p, 0)
                if z is not None:
                    p_transposes(z, 0)
                if w is not None:
                    scores(w, p, 1)
                if z is not None:
                    outputs(z, 1 - p, 0)
                if u is not None:
                    x_transposes(u, p)
                if z is not None:
                    p_transposes(z, 1)
                    outputs(z, 1 - p, 1)
                if u is not None:
                    qk_products(u, p)
                if z is not None:
                    projection(z, 0)
                    projection(z, 1)
                if c is not None:
                    v_products(c, 1 - p)

            skewed(pe, UNITS, LAG, START, body)

        @block.scalar
        def _(act):
            act.wait_ge(zeroed, 4)

            def copy_xT(u, p):
                act.wait_ge(xT_mm, u + 1)
                need(act, v_mm, u - 1)
                nc.scalar.copy(xT[p][:], ps_x).then_inc(xT_sb, 1)

            def copy_qk(u, p):
                act.wait_ge(qk_mm, u + 1)
                need(act, s_mm[1], u - 1)
                need(act, conv_done, 4 * (u - 1))
                need(act, pool_conv, 2 * (u - 1))
                nc.scalar.activation(qT[p][:], ps_qk[:, 0:256], ACT.Identity, bias=consts["bq"][:],
                                     scale=scale).then_inc(q_sb, 1)
                nc.scalar.activation(kpad[p][:, :, 1:S + 1],
                                     ps_qk[:, 256:512].rearrange("p (b k) -> p b k", b=NB), ACT.Identity,
                                     bias=consts["bk"][:]).then_inc(k_sb, 1)

            def tap(u, p, g):
                if g == 0:
                    act.wait_ge(k_sb, u + 1)
                    need(act, s_mm[1], u - 1)
                for o in range(4 * g, 4 * g + 4):
                    last = nc.scalar.activation(kc[p][:, :, o, :], kpad[p][:, :, 0:S], ACT.Copy,
                                                scale=consts["cw"][:, o, 0:1])
                last.then_inc(tap_done, 1)

            def exponent(w, s):
                act.wait_ge(shift_done[s], w + 1)
                need(act, inverse_done[s], w)
                need(act, pt_mm, 4 * w - 2 + 2 * s)
                scores_of = ps_s[s].rearrange("p n (h k) -> p (n h) k", k=S)
                for h in range(H):
                    last = nc.scalar.activation(probs[s][:, h, :], scores_of[:, h, :], ACT.Exp,
                                                bias=shift[s][:, h:h + 1], accum_out=total[s][:, h:h + 1])
                last.then_inc(exp_done[s], 1)

            def copy_pT(w, s):
                for g in range(2):
                    act.wait_ge(pt_mm, 4 * w + 2 * s + g + 1)
                    if g == 0:
                        need(act, o_mm[s], w)
                    nc.scalar.copy(probsT[s][:, 4 * g:4 * g + 4, :],
                                   ps_pt.rearrange("p (j q) -> p j q", j=4)).then_inc(pt_sb, 1)

            def body(i, p):
                u, c, w, z = stage(i, 0, UNITS), stage(i, 1, UNITS), stage(i, 2, UNITS), stage(i, 3, UNITS)
                if c is not None:
                    tap(c, 1 - p, 0)
                if z is not None:
                    copy_pT(z, 0)
                if w is not None:
                    exponent(w, 0)
                if u is not None:
                    copy_xT(u, p)
                if c is not None:
                    tap(c, 1 - p, 1)
                if z is not None:
                    copy_pT(z, 1)
                if w is not None:
                    exponent(w, 1)
                if u is not None:
                    copy_qk(u, p)

            skewed(act, UNITS, LAG, START, body)

        @block.vector
        def _(dve):
            dve.wait_ge(zeroed, 4)

            def add_taps(u, p, g, t, ready, done):
                dve.wait_ge(ready, 2 * u + g % 2 + 1)
                for o in range(4 * g, 4 * g + 4):
                    last = nc.vector.scalar_tensor_tensor(
                        out=kc[p][:, :, o, :], in0=kpad[p][:, :, t:t + S], scalar=consts["cw"][:, o, t:t + 1],
                        in1=kc[p][:, :, o, :], op0=ALU.mult, op1=ALU.add)
                last.then_inc(done, 1)

            def row_top(w, s):
                dve.wait_ge(s_mm[s], w + 1)
                nc.vector.tensor_reduce(top[s][:], ps_s[s].rearrange("p n (h k) -> p (n h) k", k=S), AX.X,
                                        ALU.max).then_inc(top_done[s], 1)

            def shift_top(w, s):
                dve.drain()
                nc.vector.tensor_tensor(topb[s][:], top[s][:], consts["cb"][:], ALU.add)
                dve.drain()
                need(dve, exp_done[s], w)
                nc.vector.tensor_tensor(shift[s][:], consts["cb"][:], topb[s][:],
                                        ALU.subtract).then_inc(shift_done[s], 1)

            def invert(w, s):
                dve.wait_ge(exp_done[s], w + 1)
                need(dve, norm_done[s], w)
                nc.vector.reciprocal(inverse[s][:], total[s][:]).then_inc(inverse_done[s], 1)

            def copy_outputs(w, s):
                dve.wait_ge(o_mm[s], w + 1)
                need(dve, a_mm[s], w)
                nc.vector.tensor_copy(outT[s][:].rearrange("p n q -> p (n q)"), ps_vo[:, 0:256]).then_inc(o_sb[s], 1)

            def layernorm_stats(w):
                dve.wait_ge(a_mm[1], w + 1)
                dve.wait_ge(a_mm[0], w + 1)
                dve.wait_ge(xb_done, w + 1)
                nc.vector.tensor_tensor(res[:], ps_a, x_all[:, bass.ds(2 * w, 2), :], ALU.add).then_inc(res_done, 1)
                dve.wait_ge(res_done, w + 1)
                for s in range(2):
                    last = nc.vector.bn_stats(stats[:, s, :], res[:, s, :])
                dve.drain()
                for s in range(2):
                    last = nc.vector.bn_aggr(mv[:, s, :], stats[:, s, :])
                last.then_inc(mv_done, 1)

            def layernorm_apply(w):
                dve.wait_ge(rstd_done, w + 1)
                for s in range(2):
                    last = nc.vector.tensor_scalar(x_all[:, bass.ds(2 * w + s, 1), :].rearrange("p a e -> p (a e)"),
                                                   res[:, s, :], mv[:, s, 0:1],
                                                   rstd[:, s:s + 1], ALU.subtract, ALU.mult)
                last.then_inc(x1_done, 1)

            def v_block_diagonal(u, p):
                dve.wait_ge(v_mm, u + 1)
                need(dve, o_mm[1], u - 1)
                for h in range(2):
                    q = slice(64 * h, 64 * h + 64)
                    last = nc.vector.tensor_tensor(
                        vbd[p][q, :, :, h, :],
                        ps_vo.rearrange("p (b j h d) -> p j b h d", b=NB, h=2, d=DH)[q, :, :, h, :],
                        consts["bv"].rearrange("p (j h d) -> p j h d", h=2, d=DH)[q, :, h, :]
                        .unsqueeze(2).to_broadcast([64, PAIRS, NB, DH]), ALU.add)
                last.then_inc(v_sb, 1)

            def body(i, p):
                c, w, z = stage(i, 1, UNITS), stage(i, 2, UNITS), stage(i, 3, UNITS)

                if w is not None:
                    row_top(w, 0)
                    shift_top(w, 0)
                if c is not None:
                    add_taps(c, 1 - p, 0, 1, tap_done, mid_done)
                    add_taps(c, 1 - p, 0, 2, mid_done, conv_done)
                if w is not None:
                    row_top(w, 1)
                    shift_top(w, 1)
                if z is not None:
                    copy_outputs(z, 0)
                if c is not None:
                    add_taps(c, 1 - p, 2, 1, pool_taps, conv_done)
                    add_taps(c, 1 - p, 3, 1, pool_taps, conv_done)
                if w is not None:
                    invert(w, 0)
                if z is not None:
                    copy_outputs(z, 1)
                if c is not None:
                    add_taps(c, 1 - p, 1, 1, tap_done, mid_done)
                    add_taps(c, 1 - p, 1, 2, mid_done, conv_done)
                if z is not None:
                    layernorm_stats(z)
                if c is not None:
                    v_block_diagonal(c, 1 - p)
                if z is not None:
                    layernorm_apply(z)
                if w is not None:
                    invert(w, 1)

            skewed(dve, UNITS, LAG, START, body)


def prepare(nc, ps, consts, dram, w_all):
    with ExitStack() as ctx:
        def tile(name, shape, dt=F32):
            return ctx.enter_context(nc.sbuf_tensor(name, shape, dt))

        def sem(name):
            return ctx.enter_context(nc.semaphore("p_" + name))

        natural = tile("attn_natural", [P, 4, D])
        gate_w = tile("gate_natural", [E, D])
        wo_wide = tile("wo_wide", [P, BT, 2, 4, BT, 2 * DH])
        bqs = tile("biases_q", [P, 2])
        places = tile("places", [P, T, TOP], mybir.dt.int32)
        counts = tile("counts", [P, NT], mybir.dt.int32)
        staged = [tile(f"staged{m}", [P, 4, P]) for m in range(3)]

        small = sem("small")
        taps_w = sem("taps_w")
        attn_w = sem("attn_w")
        cross_w = sem("cross_w")
        zero, identity_made, wide_made = sem("zero"), sem("identity"), sem("wide")
        ready = consts["ready"]
        turned, copied = sem("turned"), sem("copied")
        wide_turned = sem("wide_turned")
        landed = [sem(f"landed{m}") for m in range(3)]
        w_turned = [sem(f"w_turned{m}") for m in range(3)]
        w_copied = [sem(f"w_copied{m}") for m in range(3)]

        block = ctx.enter_context(nc.Block())

        def row(ap):
            return ap.unsqueeze(0).to_broadcast([P] + list(ap.shape))

        def column(ap):
            return ap.unsqueeze(1)

        @block.sync
        def _(sp):
            for n, name in enumerate(("Wq", "Wk", "Wv", "Wo")):
                sp.dma_start(natural[:, n, :], dram["L0_attn_" + name]).then_inc(attn_w, 16)
            sp.dma_start(gate_w[:], dram["L0_ffn_gate_w"]).then_inc(attn_w, 16)
            for name, to in (("Wq", "xwq"), ("Wk", "xwk"), ("Wv", "xwv")):
                sp.dma_start(consts[to][:], dram["L0_xattn_" + name]).then_inc(cross_w, 16)
            sources = [dram["L0_ffn_w1"].rearrange("e (c f) h -> f e c h", c=4),
                       dram["L0_ffn_w3"].rearrange("e (c f) h -> f e c h", c=4),
                       dram["L0_ffn_w2"].rearrange("e h (c f) -> h e c f", c=4)]


            def load_weights(e):
                for m in range(3):
                    need(sp, landed[m], 16 * e)
                    need(sp, w_turned[m], e)
                    sp.dma_start(staged[m][:], sources[m][:, bass.ds(e, 1), :, :].rearrange("p a c h -> p (a c) h")
                                 ).then_inc(landed[m], 16)

            load_weights(0)
            with sp.Fori(1, E) as e:
                load_weights(e)
            sp.wait_ge(cross_w, 48)

        @block.scalar
        def _(act):
            for name, to in (("L0_attn_bo", "bo"), ("L0_attn_bv", "bv"), ("L0_xattn_bv", "xbv")):
                act.dma_start(consts[to], row(dram[name])).then_inc(small, 16)
            act.dma_start(bqs[:, 0:1], column(dram["L0_attn_bq"])).then_inc(small, 16)
            act.dma_start(bqs[:, 1:2], column(dram["L0_xattn_bq"])).then_inc(small, 16)
            act.dma_start(consts["bk"], column(dram["L0_attn_bk"])).then_inc(small, 16)
            act.dma_start(consts["xbk"], column(dram["L0_xattn_bk"])).then_inc(small, 16)
            act.dma_start(consts["cb"], row(dram["L0_attn_conv_b"])).then_inc(small, 16)
            for i in range(H):
                act.dma_start(consts["cw"][DH * i:DH * i + DH, :, :],
                               dram["L0_attn_conv_w"][:, i, :].unsqueeze(0).to_broadcast([DH, H, KS])
                               ).then_inc(taps_w, 16)
            act.wait_ge(small, 8 * 16)
            act.wait_ge(taps_w, H * 16)
            nc.scalar.mul(consts["bq"], bqs[:, 0:1], 1.0 / float(np.sqrt(np.float32(DH))))
            nc.scalar.mul(consts["xbq"], bqs[:, 1:2], 1.0 / float(np.sqrt(np.float32(D)))).then_inc(ready, 1)
            act.wait_ge(turned, 5)
            for n, to in enumerate(("wqT", "wkT", "wvT")):
                nc.scalar.copy(consts[to][:], ps[:, n, 0:P])
            nc.scalar.copy(consts["gateT"][:], ps[:, 3, 0:E]).then_inc(copied, 1)
            act.wait_ge(wide_turned, 1)
            nc.scalar.copy(consts["woP"][:].rearrange("p b n e -> p (b n e)"), ps[:, 4, :]).then_inc(copied, 1)
            with act.Fori(0, E) as e:
                for m in range(3):
                    act.wait_ge(w_turned[m], e + 1)
                    nc.scalar.copy(w_all[:, bass.ds(e * (3 * F) + m * F, F)], ps[:, 5 + m, :]).then_inc(w_copied[m], 1)

        @block.gpsimd
        def _(pool):
            nc.gpsimd.memset(consts["ident"][:], 0.0).then_inc(zero, 1)
            nc.gpsimd.memset(consts["mhalf"][:], -0.5)
            nc.gpsimd.memset(consts["eps"][:], EPS)
            nc.gpsimd.memset(wo_wide[:], 0.0).then_inc(zero, 1)
            nc.gpsimd.memset(consts["ones_b"][:], 1.0).then_inc(zero, 1)
            nc.gpsimd.iota(places[:], pattern=[[TOP * P, T], [1, TOP]], base=0, channel_multiplier=TOP)
            nc.gpsimd.iota(counts[:], pattern=[[1, NT]], base=0, channel_multiplier=0).then_inc(zero, 1)
            pool.wait_ge(zero, 4)
            nc.gpsimd.affine_select(out=consts["ident"][:], in_=consts["ident"][:], compare_op=ALU.not_equal,
                                    fill=1.0, base=0, pattern=[[-1, P]], channel_multiplier=1
                                    ).then_inc(identity_made, 1)
            nc.gpsimd.affine_select(out=consts["below_b"][:], in_=consts["ones_b"][:], compare_op=ALU.is_gt,
                                    fill=0.0, base=0, pattern=[[1, P]], channel_multiplier=-1)
            pool.wait_ge(attn_w, 80)
            for b in range(BT):
                last = nc.gpsimd.tensor_copy(
                    wo_wide[:, b, :, :, b, :],
                    natural[:, 3, :].rearrange("p (n j c) -> p n j c", n=2, j=4))
            last.then_inc(wide_made, 1)

        @block.vector
        def _(dve):
            for h in range(2):
                for g in range(2):
                    last = nc.vector.memset(consts["pair_ones"][64 * h:64 * h + 64, :, g, :], float(h == g))
            dve.wait_ge(zero, 4)
            nc.vector.tensor_copy(consts["tokens"][:], places[:])
            nc.vector.tensor_copy(consts["numbers"][:], counts[:])
            nc.vector.tensor_copy(consts["experts"][:], counts[:, 0:E])
            for e in range(E):
                nc.vector.memset(consts["upto"][:, e, 0:e + 1], 1.0)
                if e < E - 1:
                    nc.vector.memset(consts["upto"][:, e, e + 1:], 0.0)
            dve.drain().then_inc(ready, 1)

        @block.tensor
        def _(pe):
            ident = consts["ident"]
            pe.wait_ge(identity_made, 1)
            pe.wait_ge(attn_w, 80)
            for n in range(3):
                nc.tensor.transpose(ps[:, n, 0:P], natural[:, n, :], ident[:]).then_inc(turned, 1)
            nc.tensor.transpose(ps[:, 3, 0:E], gate_w[:], ident[0:E, 0:E]).then_inc(turned, 2)
            pe.wait_ge(wide_made, 1)
            for b in range(BT):
                for n in range(2):
                    last = nc.tensor.transpose(ps[:, 4, (2 * b + n) * P:(2 * b + n + 1) * P],
                                               wo_wide[:, b, n, :, :, :], ident[:])
            last.then_inc(wide_turned, 1)

            def turn_weights(e):
                for m in range(3):
                    pe.wait_ge(landed[m], 16 * e + 16)
                    need(pe, w_copied[m], e)
                    for c in range(4):
                        last = nc.tensor.transpose(ps[:, 5 + m, c * P:(c + 1) * P], staged[m][:, c, :], ident[:])
                    last.then_inc(w_turned[m], 1)

            turn_weights(0)
            with pe.Fori(1, E) as e:
                turn_weights(e)


def cross_attention(nc, ps, consts, dram, x_all, rows, carried):
    TG = 4
    UNITS = T // TG
    PR = TG // 2
    W = TG * P
    LAG, START = 5, 8
    scale = 1.0 / float(np.sqrt(np.float32(D)))

    with ExitStack() as ctx:
        def tile(name, shape, dt=F32):
            return ctx.enter_context(nc.sbuf_tensor(name, shape, dt))

        def sem(name):
            return ctx.enter_context(nc.semaphore("x" + name))

        x1 = [tile(f"x1_{p}", [P, TG, D]) for p in range(2)]
        cin = [tile(f"ctx_in{p}", [P, TG, D]) for p in range(2)]
        x1T = [tile(f"x1T{p}", [P, W]) for p in range(2)]
        cT = [tile(f"ctxT{p}", [P, W]) for p in range(2)]
        qT = [tile(f"xqT{p}", [P, W]) for p in range(2)]
        kT = [tile(f"xkT{p}", [P, W]) for p in range(2)]
        v = [tile(f"xv{p}", [P, PR, BT, D]) for p in range(2)]
        probs = [tile(f"xprobs{p}", [P, TG, S]) for p in range(2)]
        weights = [tile(f"xweights{p}", [P, TG, S]) for p in range(2)]
        probsT = tile("xprobsT", [P, PR, P])
        top = tile("xtop", [P, TG])
        total = tile("xtotal", [P, TG])
        inverse = tile("xinverse", [P, TG])
        res = tile("xres", [P, TG, D])
        stats = tile("xstats", [P, TG, 6])
        mv = tile("xmv", [P, TG, 2])
        veps = tile("xveps", [P, TG])
        rstd = tile("xrstd", [P, TG])
        x2 = [tile(f"x2_{p}", [P, TG, D]) for p in range(2)]
        x2T = tile("x2T", [P, W])
        gates = tile("gates", [P, TG, E])
        ordered = tile("ordered", [P, TG, E + 1])
        absolute = tile("absolute", [P, TG, E + 1])
        place = tile("place", [P, TG, E], U32)
        region = tile("region", [P, TG, TOP])
        placef = tile("placef", [P, TG, TOP])
        gap = tile("gap", [P, TG, TOP, E])
        size = tile("size", [P, TG, TOP, E])
        near = tile("near", [P, TG, TOP, E])
        powers = tile("powers", [P, TG, TOP, E])
        kept = tile("kept", [P, TG, TOP, E])
        power_sum = tile("power_sum", [P, TG, TOP])
        chosen = tile("chosen", [P, TG, TOP, E])
        both = tile("both", [P, TG, E])
        both_b = tile("both_b", [P, TG, E], BF16)
        unit_sum = tile("unit_sum", [P, E])
        carried_b = tile("carried_b", [P, E], BF16)
        picked = tile("picked", [P, TG, TOP, E])
        offset = tile("offset", [P, TG, TOP])
        target = tile("target", [P, TG, TOP], U32)
        zeros = tile("xzeros", [P, TG, TOP], U32)
        to = [tile(f"to{p}", [P, TG, TOP], U32) for p in range(2)]
        row = [tile(f"row{p}", [P, TG, TOP, RW]) for p in range(2)]

        ps_xt, ps_ct, ps_q, ps_k, ps_v = (ps[:, n, :] for n in range(5))
        ps_s = ps[:, 5, 0:256].rearrange("p (t k) -> p t k", t=TG)
        ps_g = ps[:, 5, 448:480].rearrange("p (t e) -> p t e", t=TG)
        ps_r = ps[:, 7, 448:480].rearrange("p (t e) -> p t e", t=TG)
        ps_o = ps[:, 6:8, 0:256].rearrange("p h (r e) -> p r h e", r=PR)
        ps_pt = ps[:, 6, 256:512].rearrange("p (r q) -> p r q", r=PR)

        ctx_landed = [sem(f"ctx_landed{p}") for p in range(2)]
        x1_done = sem("x1_done")
        xt_mm, x1T_sb, ct_mm, cT_sb = sem("xt_mm"), sem("x1T_sb"), sem("ct_mm"), sem("cT_sb")
        q_mm, q_sb, k_mm, k_sb, v_mm, v_sb = (sem(n) for n in ("q_mm", "q_sb", "k_mm", "k_sb", "v_mm", "v_sb"))
        s_mm, top_done, sub_done, exp_done = (sem(n) for n in ("s_mm", "top_done", "sub_done", "exp_done"))
        total_done, inverse_done, weights_done = (sem(n) for n in ("total_done", "inverse_done", "weights_done"))
        pt_mm, pt_sb, o_mm, res_done = (sem(n) for n in ("pt_mm", "pt_sb", "o_mm", "res_done"))
        mv_done, veps_done, rstd_done = (sem(n) for n in ("mv_done", "veps_done", "rstd_done"))
        x2_done, x2t_mm, x2T_sb, gate_mm, gate_sb = (
            sem(n) for n in ("x2_done", "x2t_mm", "x2T_sb", "gate_mm", "gate_sb"))
        x2_kept, zeroed = sem("x2_kept"), sem("zeroed")
        r_step, gap_done, powers_done, weight_done = sem("r_step"), sem("gap"), sem("powers"), sem("weight")
        both_done, rank_mm, to_done, row_x, row_id = sem("both"), sem("rank_mm"), sem("to"), sem("row_x"), sem("row_id")
        scattered, rank_read, offset_done = sem("scattered"), sem("rank_read"), sem("offset")

        ctx_tiles = dram["ctx_1024"].rearrange("(t b) s e -> (b s) t e", b=BT)
        block = ctx.enter_context(nc.Block())

        @block.sync
        def _(sp):
            def load(u, p):
                need(sp, ct_mm, u - 1)
                sp.dma_start(cin[p][:], ctx_tiles[:, bass.ds(TG * u, TG), :]).then_inc(ctx_landed[p], 16)

            for u in range(4):
                load(u, u % 2)
            with sp.Fori(2, UNITS // 2) as two:
                for p in range(2):
                    load(2 * two + p, p)

        @block.gpsimd
        def _(pool):
            def rsqrt(w):
                pool.wait_ge(mv_done, w + 1)
                nc.gpsimd.tensor_tensor(veps[:], mv[:, :, 1], consts["eps"][:, 0:mv.shape[1]], ALU.add).then_inc(veps_done, 1)
                pool.wait_ge(veps_done, w + 1)
                nc.gpsimd.tensor_tensor(rstd[:], veps[:], consts["mhalf"][:, 0:TG], ALU.pow).then_inc(rstd_done, 1)

            def scatter(w, p):
                pool.wait_ge(row_x, 2 * w + 2)
                pool.wait_ge(row_id, w + 1)
                pool.wait_ge(weight_done, w + 1)
                pool.wait_ge(offset_done, w + 1)
                need(pool, scattered, 128 * (w - 1))
                nc.gpsimd.tensor_tensor(to[p][:], target[:], zeros[:], ALU.add).then_inc(to_done, 1)
                pool.drain()
                for t in range(TG):
                    for n in range(TOP):
                        pool.indirect_dma_start(rows, bass.IndirectOffsetOnAxis(to[p][:, t, n:n + 1], 0),
                                                row[p][:, t, n, :], None).then_inc(scattered, 16)

            def body(i, p):
                if (w := stage(i, 3, UNITS)) is not None:
                    rsqrt(w)
                if (w := stage(i, 5, UNITS)) is not None:
                    scatter(w, 1 - p)

            nc.gpsimd.memset(zeros[:], 0)
            pool.drain()
            skewed(pool, UNITS, LAG, START, body)

        @block.tensor
        def _(pe):
            ident = consts["ident"]

            def x_transposes(u, p):
                pe.wait_ge(x1_done, u + 1)
                need(pe, x1T_sb, u)
                for t in range(TG):
                    last = nc.tensor.transpose(ps_xt[:, t * P:(t + 1) * P], x1[p][:, t, :], ident[:])
                last.then_inc(xt_mm, 1)

            def ctx_transposes(u, p):
                pe.wait_ge(ctx_landed[p], 8 * (u - p) + 16)
                need(pe, cT_sb, u)
                need(pe, x2T_sb, u - 4)
                for t in range(TG):
                    last = nc.tensor.transpose(ps_ct[:, t * P:(t + 1) * P], cin[p][:, t, :], ident[:])
                last.then_inc(ct_mm, 1)

            def products(u, p):
                pe.wait_ge(x1T_sb, u + 1)
                need(pe, q_sb, u)
                nc.tensor.matmul(ps_q, consts["xwq"][:], x1T[p][:], start=True, stop=True).then_inc(q_mm, 1)
                pe.wait_ge(cT_sb, u + 1)
                need(pe, k_sb, u)
                nc.tensor.matmul(ps_k, consts["xwk"][:], cT[p][:], start=True, stop=True).then_inc(k_mm, 1)
                need(pe, v_sb, u)
                for r in range(PR):
                    for b in range(BT):
                        for h in range(2):
                            c = (2 * r + h) * P + b * S
                            last = nc.tensor.matmul(ps_v[64 * h:64 * h + 64, (BT * r + b) * D:(BT * r + b + 1) * D],
                                                    cT[p][:, c:c + S], consts["xwv"][:], start=True, stop=True)
                last.then_inc(v_mm, 1)

            def scores(w, p):
                pe.wait_ge(q_sb, w + 1)
                pe.wait_ge(k_sb, w + 1)
                need(pe, sub_done, w)
                need(pe, gate_sb, w - 2)
                for t in range(TG):
                    for b in range(BT):
                        c = slice(t * P + b * S, t * P + (b + 1) * S)
                        last = nc.tensor.matmul(ps_s[64 * b:64 * b + 64, t, :], qT[p][:, c], kT[p][:, c],
                                                start=True, stop=True)
                last.then_inc(s_mm, 1)

            def p_transposes(w, p):
                pe.wait_ge(weights_done, w + 1)
                need(pe, pt_sb, w)
                need(pe, res_done, w)
                need(pe, rank_read, w - 2)
                for r in range(PR):
                    last = nc.tensor.transpose(ps_pt[:, r, :], weights[p][:, 2 * r:2 * r + 2, :], ident[:])
                last.then_inc(pt_mm, 1)

            def outputs_ready(w):
                pe.wait_ge(pt_sb, w + 1)
                pe.wait_ge(v_sb, w + 1)

            def outputs(w, p):
                for r in range(PR):
                    for b in range(BT):
                        for h in range(2):
                            k = slice(64 * h, 64 * h + 64)
                            last = nc.tensor.matmul(ps_o[64 * b:64 * b + 64, r, h, :],
                                                    probsT[k, r, b * S:(b + 1) * S], v[p][k, r, b, :],
                                                    start=True, stop=True)
                last.then_inc(o_mm, 1)

            def x2_transposes(w, p):
                pe.wait_ge(x2_done, w + 1)
                pe.wait_ge(cT_sb, upto(w + 5, UNITS))
                for t in range(TG):
                    last = nc.tensor.transpose(ps_ct[:, t * P:(t + 1) * P], x2[p][:, t, :], ident[:])
                last.then_inc(x2t_mm, 1)

            def gate(w):
                pe.wait_ge(x2T_sb, w + 1)
                pe.wait_ge(sub_done, upto(w + 3, UNITS))
                need(pe, gate_sb, w)
                for t in range(TG):
                    last = nc.tensor.matmul(ps_g[:, t, :], x2T[:, t * P:(t + 1) * P], consts["gateT"][:],
                                            start=True, stop=True)
                last.then_inc(gate_mm, 1)

            def ranks(w):
                pe.wait_ge(both_done, w + 1)
                pe.wait_ge(res_done, upto(w + 3, UNITS))
                need(pe, rank_read, w)
                nc.tensor.matmul(ps_r, consts["ones_b"][:], carried_b[:].unsqueeze(1).to_broadcast([P, TG, E]),
                                 start=True, stop=False, skip_group_check=True)
                for t in range(TG - 1):
                    nc.tensor.matmul(ps_r[:, t + 1:, :], consts["ones_b"][:],
                                     both_b[:, t:t + 1, :].to_broadcast([P, TG - 1 - t, E]),
                                     start=False, stop=False, skip_group_check=True)
                nc.tensor.matmul(ps_r, consts["below_b"][:], both_b[:], start=False, stop=True,
                                 skip_group_check=True).then_inc(rank_mm, 1)

            def body(i, p):
                if (w := stage(i, 2, UNITS)) is not None:
                    scores(w, p)
                if (u := stage(i, 0, UNITS)) is not None:
                    x_transposes(u, p)
                    ctx_transposes(u, p)
                if (w := stage(i, 3, UNITS)) is not None:
                    p_transposes(w, 1 - p)
                if (u := stage(i, 1, UNITS)) is not None:
                    products(u, 1 - p)
                if (w := stage(i, 3, UNITS)) is not None:
                    outputs_ready(w)
                if (w := stage(i, 4, UNITS)) is not None:
                    x2_transposes(w, p)
                if (w := stage(i, 3, UNITS)) is not None:
                    outputs(w, 1 - p)
                if (w := stage(i, 4, UNITS)) is not None:
                    gate(w)
                if (w := stage(i, 5, UNITS)) is not None:
                    ranks(w)

            skewed(pe, UNITS, LAG, START, body)

        @block.scalar
        def _(act):
            def fetch_x1(u, p):
                need(act, xt_mm, u - 1)
                nc.scalar.copy(x1[p][:], x_all[:, bass.ds(TG * u, TG), :]).then_inc(x1_done, 1)

            def keep_x2(w, p):
                act.wait_ge(x2_done, w + 1)
                nc.scalar.copy(x_all[:, bass.ds(TG * w, TG), :], x2[p][:]).then_inc(x2_kept, 1)

            def copy_xT(u, p):
                act.wait_ge(xt_mm, u + 1)
                need(act, q_mm, u - 1)
                nc.scalar.copy(x1T[p][:], ps_xt).then_inc(x1T_sb, 1)
                act.wait_ge(ct_mm, u + 1)
                need(act, v_mm, u - 1)
                nc.scalar.copy(cT[p][:], ps_ct).then_inc(cT_sb, 1)

            def copy_qk(u, p):
                act.wait_ge(q_mm, u + 1)
                need(act, s_mm, u - 1)
                nc.scalar.activation(qT[p][:], ps_q, ACT.Identity, bias=consts["xbq"][:],
                                     scale=scale).then_inc(q_sb, 1)
                act.wait_ge(k_mm, u + 1)
                nc.scalar.activation(kT[p][:], ps_k, ACT.Identity, bias=consts["xbk"][:]).then_inc(k_sb, 1)

            def exponent(w, p):
                act.wait_ge(sub_done, w + 1)
                nc.scalar.activation(probs[p][:], probs[p][:], ACT.Exp).then_inc(exp_done, 1)

            def copy_pT(w):
                act.wait_ge(pt_mm, w + 1)
                need(act, o_mm, w)
                nc.scalar.copy(probsT[:], ps_pt).then_inc(pt_sb, 1)

            def copy_x2T(w):
                act.wait_ge(x2t_mm, w + 1)
                need(act, gate_mm, w)
                nc.scalar.copy(x2T[:], ps_ct).then_inc(x2T_sb, 1)

            def fill_rows(w, p):
                act.wait_ge(x2_kept, w + 1)
                need(act, scattered, 128 * (w - 1))
                for n in range(TOP):
                    nc.scalar.copy(row[p][:, :, n, 0:D], x_all[:, bass.ds(TG * w, TG), :]).then_inc(row_x, 1)

            def powers_of_gap(w):
                act.wait_ge(gap_done, w + 1)
                need(act, weight_done, w)
                nc.scalar.activation(powers[:], gap[:], ACT.Exp).then_inc(powers_done, 1)

            def body(i, p):
                if (u := stage(i, 0, UNITS)) is not None:
                    copy_xT(u, p)
                if (w := stage(i, 2, UNITS)) is not None:
                    exponent(w, p)
                if (w := stage(i, 3, UNITS)) is not None:
                    copy_pT(w)
                if (u := stage(i, 1, UNITS)) is not None:
                    copy_qk(u, 1 - p)
                if (w := stage(i, 5, UNITS)) is not None:
                    powers_of_gap(w)
                    fill_rows(w, 1 - p)
                if (w := stage(i, 4, UNITS)) is not None:
                    copy_x2T(w)
                if (u := stage(i, -1, UNITS)) is not None:
                    fetch_x1(u, 1 - p)
                if (w := stage(i, 3, UNITS)) is not None:
                    keep_x2(w, 1 - p)

            fetch_x1(0, 0)
            skewed(act, UNITS, LAG, START, body, ahead=1)

        @block.vector
        def _(dve):
            nc.vector.memset(ordered[:, :, E:E + 1], -3.0e38)
            nc.vector.memset(carried[:], 0.0)
            dve.drain()
            from_choice, absolute_from_choice = (
                bass.AP(of, 0, [[TG * (E + 1), P], [E + 1, TG], [1, TOP], [1, E]]) for of in (ordered, absolute))

            def bias_v(u, p):
                dve.wait_ge(v_mm, u + 1)
                need(dve, o_mm, u - 1)
                nc.vector.tensor_tensor(v[p][:].rearrange("p r b e -> p (r b) e"),
                                        ps_v.rearrange("p (n e) -> p n e", e=D),
                                        consts["xbv"].unsqueeze(1).to_broadcast([P, TG, D]),
                                        ALU.add).then_inc(v_sb, 1)

            def subtract_top(w, p):
                dve.wait_ge(s_mm, w + 1)
                nc.vector.tensor_reduce(top[:], ps_s, AX.X, ALU.max).then_inc(top_done, 1)
                dve.wait_ge(top_done, w + 1)
                nc.vector.tensor_tensor(probs[p][:], ps_s, top[:].unsqueeze(2).to_broadcast([P, TG, S]),
                                        ALU.subtract).then_inc(sub_done, 1)

            def normalise(w, p):
                dve.wait_ge(exp_done, w + 1)
                nc.vector.tensor_reduce(total[:], probs[p][:], AX.X, ALU.add).then_inc(total_done, 1)
                dve.wait_ge(total_done, w + 1)
                nc.vector.reciprocal(inverse[:], total[:]).then_inc(inverse_done, 1)
                dve.wait_ge(inverse_done, w + 1)
                need(dve, pt_mm, w - 1)
                nc.vector.tensor_tensor(weights[p][:], probs[p][:],
                                        inverse[:].unsqueeze(2).to_broadcast([P, TG, S]),
                                        ALU.mult).then_inc(weights_done, 1)

            def layernorm_stats(w):
                dve.wait_ge(o_mm, w + 1)
                nc.vector.tensor_tensor(res[:].rearrange("p (r h) e -> p r h e", h=2), ps_o,
                                        x_all[:, bass.ds(w * TG, TG), :].rearrange("p (r h) e -> p r h e", h=2),
                                        ALU.add).then_inc(res_done, 1)
                dve.wait_ge(res_done, w + 1)
                for t in range(TG):
                    last = nc.vector.bn_stats(stats[:, t, :], res[:, t, :])
                dve.drain()
                for t in range(TG):
                    last = nc.vector.bn_aggr(mv[:, t, :], stats[:, t, :])
                last.then_inc(mv_done, 1)

            def layernorm_apply(w, p):
                dve.wait_ge(rstd_done, w + 1)
                need(dve, x2t_mm, w - 1)
                need(dve, x2_kept, w - 1)
                for t in range(TG):
                    last = nc.vector.tensor_scalar(x2[p][:, t, :], res[:, t, :], mv[:, t, 0:1], rstd[:, t:t + 1],
                                                   ALU.subtract, ALU.mult)
                last.then_inc(x2_done, 1)

            def copy_gate(w):
                dve.wait_ge(gate_mm, w + 1)
                nc.vector.tensor_copy(gates[:], ps_g).then_inc(gate_sb, 1)

            def order_scores(w):
                dve.drain()
                for t in range(TG):
                    nc.vector.max(ordered[:, t, 0:E], gates[:, t, :])
                dve.drain()
                for t in range(TG):
                    nc.vector.max_index(place[:, t, :], ordered[:, t, 0:E], gates[:, t, :])

            def near_scores(w):
                dve.drain()
                top_n = ordered[:, :, 0:TOP].unsqueeze(3).to_broadcast([P, TG, TOP, E])
                nc.vector.tensor_tensor(gap[:], from_choice, top_n, ALU.subtract).then_inc(gap_done, 1)
                nc.vector.scalar_tensor_tensor(out=absolute[:], in0=ordered[:], scalar=-1.0, in1=ordered[:],
                                               op0=ALU.mult, op1=ALU.max)
                need(dve, to_done, w)
                nc.vector.tensor_copy(placef[:], place[:, :, 0:TOP])
                dve.drain()
                nc.vector.tensor_tensor(size[:], absolute_from_choice, top_n, ALU.max)
                dve.drain()
                nc.vector.scalar_tensor_tensor(out=near[:], in0=size[:], scalar=-2 * JITTER, in1=gap[:],
                                               op0=ALU.mult, op1=ALU.is_le)
                nc.vector.tensor_tensor(chosen[:], consts["experts"].unsqueeze(1).unsqueeze(1)
                                        .to_broadcast([P, TG, TOP, E]),
                                        placef[:].unsqueeze(3).to_broadcast([P, TG, TOP, E]), ALU.is_equal)
                dve.drain()
                nc.vector.tensor_tensor(both[:], chosen[:, :, 0, :], chosen[:, :, 1, :], ALU.add)

            def count_rows(w):
                dve.drain()
                need(dve, rank_mm, w)
                nc.vector.tensor_copy(both_b[:], both[:])
                nc.vector.tensor_copy(carried_b[:], carried[:]).then_inc(both_done, 1)
                nc.vector.tensor_reduce(unit_sum[:], both[:].rearrange("p t e -> p e t"), AX.X, ALU.add)
                dve.drain()
                nc.vector.tensor_tensor(carried[:], carried[:], unit_sum[:], ALU.add)

            def mixer_weights(w, p):
                dve.wait_ge(powers_done, w + 1)
                nc.vector.tensor_tensor(kept[:], powers[:], near[:], ALU.mult)
                dve.drain()
                nc.vector.tensor_reduce(power_sum[:], kept[:], AX.X, ALU.add)
                dve.drain()
                need(dve, scattered, 128 * (w - 1))
                nc.vector.reciprocal(row[p][:, :, :, D], power_sum[:]).then_inc(weight_done, 1)
                nc.vector.tensor_copy(row[p][:, :, :, D + 1],
                                      consts["tokens"][:, bass.ds(TG * w, TG), :]).then_inc(row_id, 1)

            def row_places(w):
                dve.wait_ge(rank_mm, w + 1)
                nc.vector.tensor_tensor(picked[:], chosen[:], ps_r.unsqueeze(2).to_broadcast([P, TG, TOP, E]),
                                        ALU.mult).then_inc(rank_read, 1)
                nc.vector.tensor_scalar(region[:], placef[:], float(ROWS), None, ALU.mult)
                dve.drain()
                nc.vector.tensor_reduce(offset[:], picked[:], AX.X, ALU.add)
                dve.drain()
                nc.vector.tensor_tensor(target[:], region[:], offset[:], ALU.add).then_inc(offset_done, 1)

            def body(i, p):
                if (w := stage(i, 5, UNITS)) is not None:
                    order_scores(w)
                if (w := stage(i, 2, UNITS)) is not None:
                    subtract_top(w, p)
                if (w := stage(i, 5, UNITS)) is not None:
                    near_scores(w)
                    count_rows(w)
                if (u := stage(i, 1, UNITS)) is not None:
                    bias_v(u, 1 - p)
                if (w := stage(i, 3, UNITS)) is not None:
                    layernorm_stats(w)
                if (w := stage(i, 4, UNITS)) is not None:
                    copy_gate(w)
                if (w := stage(i, 2, UNITS)) is not None:
                    normalise(w, p)
                if (w := stage(i, 3, UNITS)) is not None:
                    layernorm_apply(w, 1 - p)
                if (w := stage(i, 5, UNITS)) is not None:
                    mixer_weights(w, 1 - p)
                    row_places(w)

            skewed(dve, UNITS, LAG, START, body)


def plan_tiles(nc, ps, consts, rows, carried, tile_row, tile_weights):
    with ExitStack() as ctx:
        def tile(name, shape, dt=F32):
            return ctx.enter_context(nc.sbuf_tensor("t_" + name, shape, dt))

        def sem(name):
            return ctx.enter_context(nc.semaphore("t_" + name))

        MT = B * S // WT
        carried_b = tile("carried_b", [P, E], BF16)
        count = tile("count", [P, E])
        pad_at = tile("pad_at", [P, E], I32)
        more = tile("more", [P, E, MT])
        limits = tile("limits", [P, MT])
        tiles = tile("tiles", [P, E])
        upto_e = tile("upto_e", [P, E, E])
        ends = tile("ends", [P, E])
        base = tile("base", [P, E])
        past = tile("past", [P, NT, E])
        expert = tile("expert", [P, NT])
        is_e = tile("is_e", [P, NT, E])
        based = tile("based", [P, NT, E])
        used = tile("used", [P, NT])
        start = tile("start", [P, NT])
        within = tile("within", [P, NT])
        padding = tile("padding", [P, WT // P, RW])
        count_mm, pad_ready, padding_made, padded = sem("count_mm"), sem("pad_ready"), sem("padding"), sem("padded")
        tables = sem("tables")
        copied = sem("copied")
        ps_c = ps[:, 0, 0:E]
        region_end = E * ROWS
        block = ctx.enter_context(nc.Block())

        def wide(ap, n=E):
            return ap.unsqueeze(2).to_broadcast([P, ap.shape[1], n])

        @block.gpsimd
        def _(pool):
            nc.gpsimd.memset(padding[:, :, 0:D + 1], 0.0).then_inc(padding_made, 1)
            nc.gpsimd.memset(padding[:, :, D + 1:], float(4 * B * S)).then_inc(padding_made, 1)

        @block.tensor
        def _(pe):
            pe.wait_ge(copied, 1)
            nc.tensor.matmul(ps_c, consts["ones_b"][:], carried_b[:], start=True, stop=True).then_inc(count_mm, 1)

        @block.sync
        def _(sp):
            sp.wait_ge(padding_made, 2)
            sp.dma_start(rows[region_end:region_end + WT, :].rearrange("(p i) c -> p i c", p=P),
                         padding[:]).then_inc(padded, 16)
            sp.wait_ge(pad_ready, 1)
            for e in range(E):
                at = sp.value_load(pad_at[0:1, e:e + 1], min_val=0, max_val=region_end - WT)
                sp.dma_start(rows[bass.ds(at, WT), :].rearrange("(p i) c -> p i c", p=P),
                             padding[:]).then_inc(padded, 16)
            sp.wait_ge(padded, 16 * (E + 1))

        @block.vector
        def _(dve):
            nc.vector.tensor_copy(carried_b[:], carried[:]).then_inc(copied, 1)
            nc.vector.tensor_scalar(limits[:], consts["numbers"][:, 0:MT], float(WT), None, ALU.mult)
            dve.wait_ge(count_mm, 1)
            nc.vector.tensor_copy(count[:], ps_c)
            dve.drain()
            nc.vector.scalar_tensor_tensor(out=pad_at[:], in0=consts["experts"], scalar=float(ROWS), in1=count[:],
                                           op0=ALU.mult, op1=ALU.add).then_inc(pad_ready, 1)
            nc.vector.tensor_tensor(more[:], wide(count[:], MT), limits[:].unsqueeze(1).to_broadcast([P, E, MT]),
                                    ALU.is_gt)
            dve.drain()
            nc.vector.tensor_reduce(tiles[:], more[:], AX.X, ALU.add)
            dve.drain()
            nc.vector.tensor_tensor(upto_e[:], consts["upto"], tiles[:].unsqueeze(1).to_broadcast([P, E, E]),
                                    ALU.mult)
            dve.drain()
            nc.vector.tensor_reduce(ends[:], upto_e[:], AX.X, ALU.add)
            dve.drain()
            nc.vector.tensor_tensor(base[:], tiles[:], ends[:], ALU.subtract)
            nc.vector.tensor_tensor(past[:], wide(consts["numbers"]), ends[:].unsqueeze(1).to_broadcast([P, NT, E]),
                                    ALU.is_ge)
            dve.drain()
            nc.vector.tensor_scalar(base[:], base[:], float(WT), None, ALU.mult)
            nc.vector.tensor_reduce(expert[:], past[:], AX.X, ALU.add)
            dve.drain()
            nc.vector.scalar_tensor_tensor(out=base[:], in0=consts["experts"], scalar=float(ROWS), in1=base[:],
                                           op0=ALU.mult, op1=ALU.add)
            nc.vector.tensor_tensor(is_e[:], wide(expert[:]), consts["experts"].unsqueeze(1)
                                    .to_broadcast([P, NT, E]), ALU.is_equal)
            dve.drain()
            nc.vector.tensor_tensor(based[:], is_e[:], base[:].unsqueeze(1).to_broadcast([P, NT, E]), ALU.mult)
            nc.vector.tensor_reduce(used[:], is_e[:], AX.X, ALU.add)
            nc.vector.tensor_scalar(within[:], consts["numbers"], float(WT), float(-region_end), ALU.mult, ALU.add)
            dve.drain()
            nc.vector.tensor_reduce(start[:], based[:], AX.X, ALU.add)
            nc.vector.tensor_tensor(within[:], within[:], used[:], ALU.mult)
            dve.drain()
            nc.vector.tensor_tensor(start[:], start[:], within[:], ALU.add)
            nc.vector.tensor_scalar(expert[:], expert[:], float(E - 1), float(3 * F), ALU.min, ALU.mult)
            dve.drain()
            nc.vector.tensor_scalar(tile_row[:], start[:], float(region_end), None, ALU.add)
            nc.vector.tensor_copy(tile_weights[:], expert[:]).then_inc(tables, 1)
            dve.wait_ge(tables, 1)


def experts(nc, ps, consts, rows, results, w_all, tile_row, tile_weights):
    CH = WT // P
    FC = F // P
    LAG, START = 3, 6
    with ExitStack() as ctx:
        def tile(name, shape, dt=F32):
            return ctx.enter_context(nc.sbuf_tensor("f_" + name, shape, dt))

        def sem(name):
            return ctx.enter_context(nc.semaphore("f_" + name))

        row = [tile(f"row{p}", [P, CH, RW]) for p in range(2)]
        w = [tile(f"w{p}", [P, 3, F]) for p in range(2)]
        xT = [tile(f"xT{p}", [P, WT]) for p in range(2)]
        weight = [tile(f"weight{p}", [P, CH]) for p in range(2)]
        place = [tile(f"place{p}", [P, CH], U32) for p in range(2)]
        to = [tile(f"to{p}", [P, CH], U32) for p in range(2)]
        zeros = tile("zeros", [P, CH], U32)
        silu = [tile(f"silu{n}", [P, WT]) for n in range(2)]
        hidden = [tile(f"hidden{n}", [P, WT]) for n in range(4)]
        y = [tile(f"y{p}", [P, CH, D]) for p in range(2)]
        landed = [sem(f"landed{p}") for p in range(2)]
        w_copied, x_mm, xT_sb, meta = sem("w_copied"), sem("x_mm"), sem("xT_sb"), sem("meta")
        h_mm, silu_done, hidden_done, y_mm, y_sb = (sem(n) for n in ("h_mm", "silu", "hidden", "y_mm", "y_sb"))
        scattered, to_done = sem("scattered"), sem("to")
        ps_1 = [ps[:, n, :] for n in range(2)]
        ps_3 = [ps[:, 2 + n, :] for n in range(2)]
        ps_y = [ps[:, 4 + n, :] for n in range(2)]
        ps_x = ps[:, 6, :]
        block = ctx.enter_context(nc.Block())

        def run(engine, body):
            skewed(engine, NT, LAG, START, body)

        @block.sync
        def _(sp):
            def body(i, p):
                if (j := stage(i, 0, NT)) is not None:
                    at = sp.value_load(tile_row[0:1, bass.ds(j, 1)], min_val=0, max_val=E * ROWS)
                    need(sp, x_mm, j - 1)
                    need(sp, meta, j - 1)
                    sp.dma_start(row[p][:], rows[bass.ds(at, WT), :].rearrange("(p i) c -> p i c", p=P)
                                 ).then_inc(landed[p], 16)

            run(sp, body)

        @block.gpsimd
        def _(pool):
            def body(i, p):
                if (j := stage(i, 3, NT)) is not None:
                    pool.wait_ge(y_sb, j + 1)
                    need(pool, scattered, 16 * CH * (j - 1))
                    nc.gpsimd.tensor_tensor(to[1 - p][:], place[1 - p][:], zeros[:], ALU.add).then_inc(to_done, 1)
                    pool.drain()
                    for c in range(CH):
                        pool.indirect_dma_start(results, bass.IndirectOffsetOnAxis(to[1 - p][:, c:c + 1], 0),
                                                y[1 - p][:, c, :], None, bounds_check=TOP * B * S - 1,
                                                oob_is_err=False).then_inc(scattered, 16)

            nc.gpsimd.memset(zeros[:], 0)
            pool.drain()
            run(pool, body)
            pool.wait_ge(scattered, 16 * CH * NT)

        @block.tensor
        def _(pe):
            def x_transposes(j, p):
                pe.wait_ge(landed[p], 8 * (j - p) + 16)
                need(pe, xT_sb, j)
                for c in range(CH):
                    last = nc.tensor.transpose(ps_x[:, c * P:(c + 1) * P], row[p][:, c, 0:D], consts["ident"][:])
                last.then_inc(x_mm, 1)

            def hidden_products(j, p, f):
                if f == 0:
                    pe.wait_ge(xT_sb, j + 1)
                    pe.wait_ge(w_copied, j + 1)
                need(pe, hidden_done, FC * j + f - 1)
                cols = slice(f * P, (f + 1) * P)
                nc.tensor.matmul(ps_1[f % 2], w[p][:, 0, cols], xT[p][:], start=True, stop=True)
                nc.tensor.matmul(ps_3[f % 2], w[p][:, 1, cols], xT[p][:], start=True, stop=True).then_inc(h_mm, 1)

            def output_products(j, p, f):
                pe.wait_ge(hidden_done, FC * j + f + 1)
                if f == 0:
                    need(pe, y_sb, j - 1)
                for c in range(CH):
                    last = nc.tensor.matmul(ps_y[p][:, c * D:(c + 1) * D], hidden[f][:, c * P:(c + 1) * P],
                                            w[p][:, 2, f * P:(f + 1) * P], start=(f == 0 and c == 0),
                                            stop=(f == FC - 1), skip_group_check=True)
                last.then_inc(y_mm, 1)

            def body(i, p):
                t, j, k = stage(i, 0, NT), stage(i, 1, NT), stage(i, 2, NT)
                for f in range(FC):
                    if j is not None:
                        hidden_products(j, 1 - p, f)
                    if f < 2:
                        if k is not None:
                            output_products(k, p, f + 2)
                    elif j is not None:
                        output_products(j, 1 - p, f - 2)
                    if f == 1 and t is not None:
                        x_transposes(t, p)

            run(pe, body)

        @block.scalar
        def _(act):
            def body(i, p):
                if (j := stage(i, 1, NT)) is not None:
                    for f in range(FC):
                        act.wait_ge(h_mm, FC * j + f + 1)
                        need(act, hidden_done, FC * j + f - 1)
                        nc.scalar.activation(silu[f % 2][:], ps_1[f % 2], ACT.Silu).then_inc(silu_done, 1)
                        if f == 1 and (t := stage(i, 0, NT)) is not None:
                            act.wait_ge(x_mm, t + 1)
                            need(act, h_mm, FC * (t - 1))
                            nc.scalar.copy(xT[p][:], ps_x).then_inc(xT_sb, 1)
                elif (t := stage(i, 0, NT)) is not None:
                    act.wait_ge(x_mm, t + 1)
                    nc.scalar.copy(xT[p][:], ps_x).then_inc(xT_sb, 1)

            run(act, body)

        @block.vector
        def _(dve):
            def fetch_meta(t, p):
                dve.wait_ge(landed[p], 8 * (t - p) + 16)
                need(dve, y_sb, t - 1)
                need(dve, to_done, t - 1)
                nc.vector.tensor_copy(weight[p][:], row[p][:, :, D])
                nc.vector.tensor_copy(place[p][:], row[p][:, :, D + 1]).then_inc(meta, 1)

            def fetch_weights(t, p):
                at = dve.value_load(tile_weights[0:1, bass.ds(t, 1)], min_val=0, max_val=(E - 1) * 3 * F)
                need(dve, h_mm, FC * (t - 1))
                need(dve, y_mm, FC * (t - 1))
                nc.vector.tensor_copy(w[p][:].rearrange("p m f -> p (m f)"),
                                      w_all[:, bass.ds(at, 3 * F)]).then_inc(w_copied, 1)

            def hidden_step(j, f):
                dve.wait_ge(silu_done, FC * j + f + 1)
                need(dve, y_mm, FC * (j - 1) + f + 1)
                nc.vector.tensor_tensor(hidden[f][:], ps_3[f % 2], silu[f % 2][:], ALU.mult).then_inc(hidden_done, 1)

            def scale(k, p):
                dve.wait_ge(y_mm, FC * k + FC)
                dve.wait_ge(meta, k + 1)
                need(dve, scattered, 16 * CH * (k - 1))
                nc.vector.tensor_tensor(y[p][:], ps_y[p].rearrange("p (c e) -> p c e", c=CH),
                                        weight[p][:].unsqueeze(2).to_broadcast([P, CH, D]), ALU.mult
                                        ).then_inc(y_sb, 1)

            def body(i, p):
                t, j, k = stage(i, 0, NT), stage(i, 1, NT), stage(i, 2, NT)
                for f in range(FC):
                    if j is not None:
                        hidden_step(j, f)
                    if f == 2:
                        if k is not None:
                            scale(k, p)
                        if t is not None:
                            fetch_weights(t, p)
                if t is not None:
                    fetch_meta(t, p)

            run(dve, body)


def combine(nc, consts, results, x_all, out):
    TG = 4
    UNITS = T // TG
    with ExitStack() as ctx:
        def tile(name, shape, dt=F32):
            return ctx.enter_context(nc.sbuf_tensor("c2_" + name, shape, dt))

        def sem(name):
            return ctx.enter_context(nc.semaphore("c2_" + name))

        parts = [tile(f"parts{p}", [P, TG, TOP, D]) for p in range(2)]
        res = [tile(f"res{p}", [P, TG, D]) for p in range(2)]
        done = [tile(f"done{p}", [P, TG, D]) for p in range(2)]
        stats = tile("stats", [P, TG, 6])
        mv = tile("mv", [P, TG, 2])
        veps = tile("veps", [P, TG])
        rstd = [tile(f"rstd{p}", [P, TG]) for p in range(2)]
        landed = [sem(f"landed{p}") for p in range(2)]
        stored = [sem(f"stored{p}") for p in range(2)]
        sum_done, res_done, mv_done, veps_done, rstd_done, out_done = (
            sem(n) for n in ("sum", "res", "mv", "veps", "rstd", "out"))
        part_tiles = results.rearrange("(t p n) e -> p t (n e)", p=P, n=TOP)
        out_tiles = out.rearrange("(t b) s e -> (b s) t e", b=BT)
        block = ctx.enter_context(nc.Block())

        def run(engine, body):
            skewed(engine, UNITS, 1, 4, body)

        @block.sync
        def _(sp):
            def body(i, p):
                if (u := stage(i, 0, UNITS)) is not None:
                    need(sp, sum_done, u - 1)
                    sp.dma_start(parts[p][:].rearrange("p t n e -> p t (n e)"),
                                 part_tiles[:, bass.ds(TG * u, TG), :]).then_inc(landed[p], 16)

            run(sp, body)

        @block.scalar
        def _(act):
            def body(i, p):
                if (w := stage(i, 1, UNITS)) is not None:
                    act.wait_ge(out_done, w + 1)
                    act.dma_start(out_tiles[:, bass.ds(TG * w, TG), :], done[1 - p][:]).then_inc(stored[1 - p], 16)

            run(act, body)
            for p in range(2):
                act.wait_ge(stored[p], 8 * UNITS)

        @block.gpsimd
        def _(pool):
            def body(i, p):
                if (u := stage(i, 0, UNITS)) is not None:
                    pool.wait_ge(landed[p], 8 * (u - p) + 16)
                    need(pool, out_done, u - 1)
                    nc.gpsimd.tensor_tensor(res[p][:], parts[p][:, :, 0, :], parts[p][:, :, 1, :],
                                            ALU.add).then_inc(sum_done, 1)
                if (w := stage(i, 1, UNITS)) is not None:
                    pool.wait_ge(mv_done, w + 1)
                    nc.gpsimd.tensor_tensor(veps[:], mv[:, :, 1], consts["eps"][:], ALU.add).then_inc(veps_done, 1)
                    pool.wait_ge(veps_done, w + 1)
                    need(pool, out_done, w - 1)
                    nc.gpsimd.tensor_tensor(rstd[1 - p][:], veps[:], consts["mhalf"][:],
                                            ALU.pow).then_inc(rstd_done, 1)

            run(pool, body)

        @block.vector
        def _(dve):
            def body(i, p):
                if (w := stage(i, 1, UNITS)) is not None:
                    q = 1 - p
                    dve.wait_ge(sum_done, w + 1)
                    nc.vector.tensor_tensor(res[q][:], res[q][:], x_all[:, bass.ds(TG * w, TG), :],
                                            ALU.add).then_inc(res_done, 1)
                    dve.drain()
                    for t in range(TG):
                        nc.vector.bn_stats(stats[:, t, :], res[q][:, t, :])
                    dve.drain()
                    for t in range(TG):
                        last = nc.vector.bn_aggr(mv[:, t, :], stats[:, t, :])
                    last.then_inc(mv_done, 1)
                    dve.wait_ge(rstd_done, w + 1)
                    need(dve, stored[q], 8 * (w - q))
                    for t in range(TG):
                        last = nc.vector.tensor_scalar(done[q][:, t, :], res[q][:, t, :], mv[:, t, 0:1],
                                                       rstd[q][:, t:t + 1], ALU.subtract, ALU.mult)
                    last.then_inc(out_done, 1)

            run(dve, body)


def decoder(nc, dram):
    with ExitStack() as ctx:
        def tile(name, shape, dt=F32):
            return ctx.enter_context(nc.sbuf_tensor(name, shape, dt))

        x_all = tile("x_all", [P, T, D])
        ps = ctx.enter_context(nc.psum_tensor("ps", [P, 8, 512], F32))
        w_all = tile("w_all", [P, E * 3 * F])
        rows = nc.dram_tensor("rows", (E * ROWS + WT, RW), F32, kind="Internal").ap()
        results = nc.dram_tensor("results", (TOP * B * S, D), F32, kind="Internal").ap()
        shapes = {"ident": [P, P], "bo": [P, D], "bv": [P, D], "xbv": [P, D], "bq": [P, 1], "xbq": [P, 1],
                  "bk": [P, 1], "xbk": [P, 1], "cb": [P, H], "cw": [P, H, KS], "wqT": [P, P], "wkT": [P, P],
                  "wvT": [P, P], "woP": [P, BT, 2, D], "pair_ones": [P, BT, 2, DH], "mhalf": [P, 4], "eps": [P, 4],
                  "xwq": [P, P], "xwk": [P, P], "xwv": [P, P], "gateT": [P, E],
                  "ones_b": [P, P], "below_b": [P, P], "tokens": [P, T, TOP], "numbers": [P, NT],
                  "experts": [P, E], "upto": [P, E, E]}
        consts = {n: tile("c_" + n, shape, BF16 if n.endswith("_b") else F32)[:] for n, shape in shapes.items()}
        consts["ready"] = ctx.enter_context(nc.semaphore("constants_ready"))
        prepare(nc, ps, consts, dram, w_all)
        self_attention(nc, ps, consts, dram, x_all)
        carried = tile("carried", [P, E])
        tile_row = tile("tile_row", [P, NT], I32)
        tile_weights = tile("tile_weights", [P, NT], I32)
        cross_attention(nc, ps, consts, dram, x_all, rows, carried)
        plan_tiles(nc, ps, consts, rows, carried, tile_row, tile_weights)
        experts(nc, ps, consts, rows, results, w_all, tile_row, tile_weights)
        combine(nc, consts, results, x_all, dram["out"])


_INS = ["x", "ctx_1024", "L0_attn_Wq", "L0_attn_bq", "L0_attn_Wk", "L0_attn_bk", "L0_attn_Wv", "L0_attn_bv",
        "L0_attn_Wo", "L0_attn_bo", "L0_attn_conv_w", "L0_attn_conv_b", "L0_xattn_Wq", "L0_xattn_bq",
        "L0_xattn_Wk", "L0_xattn_bk", "L0_xattn_Wv", "L0_xattn_bv", "L0_ffn_gate_w", "L0_ffn_w1", "L0_ffn_w2",
        "L0_ffn_w3"]


def kernel(**inputs):
    import concourse.bacc as bacc
    from concourse.bass_utils import run_bass_kernel_spmd

    nc = bacc.Bacc("TRN2", target_bir_lowering=False, num_devices=1)
    arrays, dram = {}, {}
    for name in _INS:
        a = np.ascontiguousarray(inputs[name])
        arrays[f"in_{name}"] = a
        dram[name] = nc.dram_tensor(f"in_{name}", a.shape, mybir.dt.from_np(a.dtype), kind="ExternalInput").ap()
    dram["out"] = nc.dram_tensor("out_0", (B, S, D), F32, kind="ExternalOutput").ap()
    decoder(nc, dram)
    result = run_bass_kernel_spmd(nc, [arrays], core_ids=[0])
    return result.results[0]["out_0"]
```
